# Optimizing a Trainium2 kernel written in Bass

```python
import numpy as np
import jax
import jax.numpy as jnp

def _softmax(x, axis=-1):
    return jax.nn.softmax(x, axis=axis)
def _gelu(x):
    return jax.nn.gelu(x, approximate=True)
def _silu(x):
    return jax.nn.silu(x)
def _sigmoid(x):
    return jax.nn.sigmoid(x)
def _layernorm(x, axis=-1, eps=1e-5):
    m = jnp.mean(x, axis=axis, keepdims=True)
    v = jnp.var(x, axis=axis, keepdims=True)
    return (x - m) / jnp.sqrt(v + eps)
def _scatter_add(tgt, idx, src, axis=0):
    return tgt.at[idx].add(src)
def _segment_sum(src, seg, n):
    return jax.ops.segment_sum(src, seg, n)

kernel_name = 'mk_conv_seq_d2_conv_nchw256_492b0d'

def setup_inputs(seed: int = 0):
    np.random.seed(seed)
    _w = jnp.asarray
    def _rec_inputs():
        import jax
        import jax.numpy as jnp
        _gk = jax.random.key(seed)
        x = -0.0002928 + 1 * jax.random.normal(jax.random.fold_in(_gk, 1), (16, 256, 32, 32), jnp.float32)
        return x
    x = _rec_inputs()
    def _L0_conv_setup():
        import jax, jax.numpy as jnp
        import numpy as np
        DIM = 256
        NUM_HEADS = 8
        HEAD_DIM = 32
        INNER = NUM_HEADS * HEAD_DIM
        EPS = 1e-05

        def layer_norm(x, gamma, beta):
            mu = jnp.mean(x, axis=-1, keepdims=True)
            var = jnp.mean(jnp.square(x - mu), axis=-1, keepdims=True)
            return (x - mu) * jax.lax.rsqrt(var + EPS) * gamma + beta
        key = jax.random.key(seed)
        ks = jax.random.split(key, 8)
        s = 0.02
        return {'x': jax.random.normal(ks[0], (16, DIM, 32, 32), dtype=jnp.float32), 'w_qkv': jax.random.normal(ks[1], (3 * INNER, DIM), dtype=jnp.float32) * s, 'w_proj': jax.random.normal(ks[2], (DIM, INNER), dtype=jnp.float32) * s, 'b_proj': jnp.zeros((DIM,), dtype=jnp.float32), 'g1': jnp.ones((DIM,), dtype=jnp.float32), 'beta1': jnp.zeros((DIM,), dtype=jnp.float32), 'g2': jnp.ones((DIM,), dtype=jnp.float32), 'beta2': jnp.zeros((DIM,), dtype=jnp.float32), 'w1': jax.random.normal(ks[3], (4 * DIM, DIM), dtype=jnp.float32) * s, 'b1': jnp.zeros((4 * DIM,), dtype=jnp.float32), 'w2': jax.random.normal(ks[4], (DIM, 4 * DIM), dtype=jnp.float32) * s, 'b2': jnp.zeros((DIM,), dtype=jnp.float32)}
    _L0_conv_all = _L0_conv_setup()
    _L0_conv_in = {k: v for k, v in _L0_conv_all.items() if k in ('w_qkv', 'w_proj', 'b_proj', 'g1', 'beta1', 'g2', 'beta2', 'w1', 'b1', 'w2', 'b2', )}
    del _L0_conv_all

    def _L1_conv_setup():
        import jax, jax.numpy as jnp
        import numpy as np
        key = jax.random.key(seed)
        ks = jax.random.split(key, 6)
        B, C, W, H = (4, 256, 64, 64)
        Ci = C // 8
        s = 0.05
        return {'x': jax.random.normal(ks[0], (B, C, W, H), dtype=jnp.float32), 'wf': jax.random.normal(ks[1], (Ci, C), dtype=jnp.float32) * s, 'bf': jnp.zeros((Ci,), dtype=jnp.float32), 'wg': jax.random.normal(ks[2], (Ci, C), dtype=jnp.float32) * s, 'bg': jnp.zeros((Ci,), dtype=jnp.float32), 'wh': jax.random.normal(ks[3], (Ci, C), dtype=jnp.float32) * s, 'bh': jnp.zeros((Ci,), dtype=jnp.float32), 'wv': jax.random.normal(ks[4], (C, Ci), dtype=jnp.float32) * s, 'bv': jnp.zeros((C,), dtype=jnp.float32), 'gamma': jax.random.normal(ks[5], (1,), dtype=jnp.float32) * 0.1}
    _L1_conv_all = _L1_conv_setup()
    _L1_conv_in = {k: v for k, v in _L1_conv_all.items() if k in ('wf', 'bf', 'wg', 'bg', 'wh', 'bh', 'wv', 'bv', 'gamma', )}
    del _L1_conv_all

    return {
        "x": x,
        "L0_conv_w_qkv": _L0_conv_in["w_qkv"],
        "L0_conv_w_proj": _L0_conv_in["w_proj"],
        "L0_conv_b_proj": _L0_conv_in["b_proj"],
        "L0_conv_g1": _L0_conv_in["g1"],
        "L0_conv_beta1": _L0_conv_in["beta1"],
        "L0_conv_g2": _L0_conv_in["g2"],
        "L0_conv_beta2": _L0_conv_in["beta2"],
        "L0_conv_w1": _L0_conv_in["w1"],
        "L0_conv_b1": _L0_conv_in["b1"],
        "L0_conv_w2": _L0_conv_in["w2"],
        "L0_conv_b2": _L0_conv_in["b2"],
        "L1_conv_wf": _L1_conv_in["wf"],
        "L1_conv_bf": _L1_conv_in["bf"],
        "L1_conv_wg": _L1_conv_in["wg"],
        "L1_conv_bg": _L1_conv_in["bg"],
        "L1_conv_wh": _L1_conv_in["wh"],
        "L1_conv_bh": _L1_conv_in["bh"],
        "L1_conv_wv": _L1_conv_in["wv"],
        "L1_conv_bv": _L1_conv_in["bv"],
        "L1_conv_gamma": _L1_conv_in["gamma"],
    }

def reference(x, L0_conv_w_qkv, L0_conv_w_proj, L0_conv_b_proj, L0_conv_g1, L0_conv_beta1, L0_conv_g2, L0_conv_beta2, L0_conv_w1, L0_conv_b1, L0_conv_w2, L0_conv_b2, L1_conv_wf, L1_conv_bf, L1_conv_wg, L1_conv_bg, L1_conv_wh, L1_conv_bh, L1_conv_wv, L1_conv_bv, L1_conv_gamma):
    import jax
    import jax.numpy as jnp
    def _L0_conv_ref(x, w_qkv, w_proj, b_proj, g1, beta1, g2, beta2, w1, b1, w2, b2):
        import jax, jax.numpy as jnp
        import numpy as np
        DIM = 256
        NUM_HEADS = 8
        HEAD_DIM = 32
        INNER = NUM_HEADS * HEAD_DIM
        EPS = 1e-05

        def layer_norm(x, gamma, beta):
            mu = jnp.mean(x, axis=-1, keepdims=True)
            var = jnp.mean(jnp.square(x - mu), axis=-1, keepdims=True)
            return (x - mu) * jax.lax.rsqrt(var + EPS) * gamma + beta
        b, c, h, w = x.shape
        s = h * w
        x_flat = x.reshape(b, c, s).transpose(0, 2, 1)
        x_ln = layer_norm(x_flat, g1, beta1)
        qkv = x_ln @ w_qkv.T
        q, k, v = jnp.split(qkv, 3, axis=-1)

        def to_heads(t):
            return t.reshape(b, s, NUM_HEADS, HEAD_DIM).transpose(0, 2, 1, 3)
        q, k, v = (to_heads(q), to_heads(k), to_heads(v))
        scores = jnp.einsum('bhqd,bhkd->bhqk', q, k) * HEAD_DIM ** (-0.5)
        attn = jax.nn.softmax(scores, axis=-1)
        out = jnp.einsum('bhqk,bhkd->bhqd', attn, v)
        out = out.transpose(0, 2, 1, 3).reshape(b, s, INNER)
        out = out @ w_proj.T + b_proj
        y = x_flat + out
        ffn = jax.nn.relu(layer_norm(y, g2, beta2) @ w1.T + b1) @ w2.T + b2
        y = y + ffn
        return y.transpose(0, 2, 1).reshape(b, c, h, w)

    def _L1_conv_ref(x, wf, bf, wg, bg, wh, bh, wv, bv, gamma):
        import jax, jax.numpy as jnp
        import numpy as np
        B, C, W, H = x.shape
        N = W * H
        xf = x.reshape(B, C, N)
        f = jnp.einsum('bcn,oc->bon', xf, wf) + bf[:, None]
        g = jnp.einsum('bcn,oc->bon', xf, wg) + bg[:, None]
        h = jnp.einsum('bcn,oc->bon', xf, wh) + bh[:, None]
        logits = jnp.einsum('bcq,bck->bqk', f, g)
        attn = jax.nn.softmax(logits, axis=-1)
        x0 = jnp.einsum('bck,bqk->bcq', h, attn)
        v = jnp.einsum('bcn,oc->bon', x0, wv) + bv[:, None]
        v = v.reshape(B, C, W, H)
        return v * gamma[0] + x

    def _gn(v, G=32, eps=1e-5):
        B_, C_, H_, W_ = v.shape
        g = v.reshape(B_, G, C_ // G, H_, W_)
        m = jnp.mean(g, axis=(2, 3, 4), keepdims=True)
        s = jnp.var(g, axis=(2, 3, 4), keepdims=True)
        return ((g - m) / jnp.sqrt(s + eps)).reshape(v.shape)

    def _ln_c(v, eps=1e-6):
        m = jnp.mean(v, axis=1, keepdims=True)
        s = jnp.var(v, axis=1, keepdims=True)
        return (v - m) / jnp.sqrt(s + eps)

    def _ln_t(v, eps=1e-5):
        m = jnp.mean(v, axis=-1, keepdims=True)
        s = jnp.var(v, axis=-1, keepdims=True)
        return (v - m) / jnp.sqrt(s + eps)

    def _to_tokens(v):
        B_, C_, H_, W_ = v.shape
        return v.reshape(B_, C_, H_ * W_).transpose(0, 2, 1)
    def _from_tokens(t, like):
        B_, C_, H_, W_ = like.shape
        return t.transpose(0, 2, 1).reshape(B_, C_, H_, W_)

    x = _L0_conv_ref(x, L0_conv_w_qkv, L0_conv_w_proj, L0_conv_b_proj, L0_conv_g1, L0_conv_beta1, L0_conv_g2, L0_conv_beta2, L0_conv_w1, L0_conv_b1, L0_conv_w2, L0_conv_b2)
    x = _L1_conv_ref(x, L1_conv_wf, L1_conv_bf, L1_conv_wg, L1_conv_bg, L1_conv_wh, L1_conv_bh, L1_conv_wv, L1_conv_bv, L1_conv_gamma)
    return x


_drawn_inputs = setup_inputs


def setup_inputs(seed=0):
    import zlib

    import numpy as np

    out = dict(_drawn_inputs(seed))
    spreads = {'L0_conv_b_proj': (0.0, 0.1),
     'L0_conv_g1': (1.0, 0.6),
     'L0_conv_beta1': (0.0, 0.8),
     'L0_conv_g2': (1.0, 0.557),
     'L0_conv_beta2': (0.0, 0.563),
     'L0_conv_b1': (0.0, 0.1),
     'L0_conv_b2': (0.0, 0.1),
     'L1_conv_bf': (0.0, 0.8),
     'L1_conv_bg': (0.0, 2.0),
     'L1_conv_bh': (0.0, 2.0),
     'L1_conv_bv': (0.0, 2.0)}
    factors = {'L0_conv_w_qkv': 5.449,
     'L0_conv_w_proj': 5.135,
     'L1_conv_wf': 7.79,
     'L1_conv_wg': 7.651,
     'L1_conv_wh': 7.099,
     'L1_conv_wv': 6.933}
    for name, (base, spread) in spreads.items():
        noise = np.random.default_rng([zlib.crc32(name.encode()), seed]).standard_normal(out[name].shape)
        drawn = base * np.exp(spread * noise) if base else spread * noise
        out[name] = jnp.asarray(drawn.astype(out[name].dtype))
    for name, factor in factors.items():
        out[name] = (out[name] * factor).astype(out[name].dtype)
    return out
```

```python
from contextlib import ExitStack

import concourse.bass as bass
from concourse import mybir

F32 = mybir.dt.float32
F32R = mybir.dt.float32r
ALU = mybir.AluOpType
ACT = mybir.ActivationFunctionType
AX = mybir.AxisListType

P = 128
DH = 32
HI, LO = 0, 1
NEG = 3 * DH
CH = 512
EPS = 1e-5
DMA = 16

V_G1, V_BETA1, V_G2, V_BETA2, V_BPROJ, V_B1, V_B2, V_BV, V_BF, V_BG, V_BH, V_GAMMA, V_COLS = (
    0, 2, 4, 6, 8, 10, 18, 20, 22, 23, 24, 25, 26)
B_QK, B_V, B_PROJ, B_FFN, B_OUT, B_COLS = 0, 4, 6, 8, 16, 18


def attention_layers(nc, x, wqkv, wproj, w1, w2, wfgh, wv, vecs, out):
    IMGS, C, N = x.shape
    CT = C // P
    KT = N // P
    NCH = N // CH
    HEADS = C // DH
    G = P // DH
    GROUPS = HEADS // G
    HID = w1.shape[1]
    HT = HID // P
    SCALE = float(DH) ** -0.5
    assert (CT, KT, NCH, G, GROUPS, HT) == (2, 8, 2, 4, 2, 8)

    JOBS = (["mean1", "var1", "q0", "k0", "vals0", "vals1", "q1", "k1", "proj0", "proj1", "mean2", "var2"]
            + [f"up0_{j}" for j in range(4)] + ["down0"] + [f"up1_{j}" for j in range(4)] + ["down1"]
            + ["f", "g", "h", "out0", "out1"])
    JOB = {name: i for i, name in enumerate(JOBS)}
    NJ = len(JOBS)
    assert NJ % 3 == 0

    STEPS = NCH * KT
    L0_HALVES = GROUPS * STEPS * 2
    HALVES = L0_HALVES + KT
    PV = GROUPS * STEPS + KT
    ITEMS = G * KT
    MAXES = GROUPS * (ITEMS * NCH + 1) + KT * NCH + 1

    with ExitStack() as ctx:
        def sb(name, shape, dt=F32):
            return ctx.enter_context(nc.sbuf_tensor(name, shape, dt))

        def sem(name):
            return ctx.enter_context(nc.semaphore(name))

        wqkv_s = sb("wqkv_s", [P, 2, CT, 3 * C], F32R)
        wproj_s = sb("wproj_s", [P, 2, CT, C], F32R)
        w1_s = sb("w1_s", [P, 2, CT, HID], F32R)
        w2_s = sb("w2_s", [P, 2, HT, C], F32R)
        wfg_s = sb("wfg_s", [P, 2, CT, 6 * DH], F32R)
        wh_s = sb("wh_s", [P, 2, CT, DH], F32R)
        wv_s = sb("wv_s", [3 * DH, C], F32R)
        vec = sb("vec", [P, V_COLS])
        bias = sb("bias", [P, B_COLS])
        avg = sb("avg", [P, P])
        ones = sb("ones", [P, DH])
        ident = sb("ident", [P, P])
        eps = sb("eps", [P, 1])
        xin = sb("xin", [P, CT, N])
        y = sb("y", [P, CT, N])
        xc = sb("xc", [P, CT, N])
        sq = sb("sq", [P, CT, N])
        act = sb("act", [P, 2, CT, N], F32R)
        stage = sb("stage", [P, 4, N], F32R)
        qs = sb("qs", [P, HEADS, N], F32R)
        ks = sb("ks", [P, HEADS, N], F32R)
        vals = sb("vals", [P, KT, C])
        vals1 = sb("vals1", [P, KT, DH])
        pr = sb("pr", [P, 4, 2, CH])
        mx = sb("mx", [P, NCH, ITEMS])
        mxc = sb("mxc", [P, ITEMS])
        negm = sb("negm", [ITEMS, P], F32R)
        hid_hi = stage[:, :, :].rearrange("p a (b c) -> p (a b) c", c=CH)
        hid_lo = qs[:, G:2 * G, :].rearrange("p a (b c) -> p (a b) c", c=CH)
        hid32 = xc
        den = sq[:, 0, 0:CH]
        quot = sq[:, 1, 0:CH]
        x0 = sq[0:DH, 1, :]
        x0s = stage[0:3 * DH, 0, :]

        maxp = ctx.enter_context(nc.psum_tensor("maxp", [P, 2, CH], F32))
        lin = ctx.enter_context(nc.psum_tensor("lin", [P, 3, 2, CH], F32))
        att_o, att_d = lin[:, 2, 0, :], lin[:, 2, 1, :]

        vec_loaded = sem("vec_loaded")
        weights_loaded = sem("weights_loaded")
        consts_zeroed = sem("consts_zeroed")
        consts_ready = sem("consts_ready")
        bias_sums = sem("bias_sums")
        bias_ready = sem("bias_ready")
        split_step = sem("split_step")
        weights_ready = sem("weights_ready")
        x_loaded = sem("x_loaded")
        job_ready = sem("job_ready")
        centred = sem("centred")
        squared = sem("squared")
        log_ready = sem("log_ready")
        guess_ready = sem("guess_ready")
        newton = sem("newton")
        rstd_ready = sem("rstd_ready")
        normed = sem("normed")
        normed_hi = sem("normed_hi")
        act_ready = sem("act_ready")
        qk_hi = sem("qk_hi")
        qk_staged = sem("qk_staged")
        q_stacked = sem("q_stacked")
        k_stacked = sem("k_stacked")
        max_scores = sem("max_scores")
        max_read = sem("max_read")
        max_ready = sem("max_ready")
        negm_placed = sem("negm_placed")
        scores_ready = sem("scores_ready")
        exp_done = sem("exp_done")
        pv_done = sem("pv_done")
        vals_ready = sem("vals_ready")
        vals1_ready = sem("vals1_ready")
        den_copied = sem("den_copied")
        num_copied = sem("num_copied")
        recip_ready = sem("recip_ready")
        quot_ready = sem("quot_ready")
        quot_hi = sem("quot_hi")
        heads_ready = sem("heads_ready")
        y_ready = sem("y_ready")
        y_free = sem("y_free")
        hid_ready = sem("hid_ready")
        hid_hi_ready = sem("hid_hi_ready")
        hid_split = sem("hid_split")
        y2_ready = sem("y2_ready")
        y2_hi = sem("y2_hi")
        y2_split = sem("y2_split")
        fg_hi = sem("fg_hi")
        fg_stacked = sem("fg_stacked")
        x0_recip = sem("x0_recip")
        x0_ready = sem("x0_ready")
        x0_hi = sem("x0_hi")
        x0_split = sem("x0_split")
        out_ready = sem("out_ready")

        def job_done(img, name):
            return img * NJ + JOB[name] + 1

        READ = {}
        for w in range(2):
            READ[f"mean{w + 1}"] = (centred, CT * (w + 1), 2 * CT)
            READ[f"var{w + 1}"] = (newton, 3 * w + 2, 6)
            READ[f"vals{w}"] = (vals_ready, w + 1, 2)
            READ[f"proj{w}"] = (y_ready, w + 1, CT)
            READ[f"down{w}"] = (y2_ready, CT * (w + 1), 2 * CT)
            READ[f"out{w}"] = (out_ready, w + 1, CT)
        for i, name in enumerate(("q0", "k0", "q1", "k1")):
            READ[name] = (qk_staged, i + 1, 4)
        for i in range(8):
            READ[f"up{i // 4}_{i % 4}"] = (hid_ready, 2 * i + 2, 16)
        READ["f"], READ["g"], READ["h"] = (fg_stacked, 1, 2), (fg_stacked, 2, 2), (vals1_ready, 1, 1)

        def wait_freed(eng, img, name):
            signal, value, per_image = READ[name]
            eng.wait_ge(signal, img * per_image + value)

        def pair(name):
            return lin[:, JOB[name] % 3, :, :]

        def items_of(s):
            over = STEPS - 3
            return range(min(s, over) * ITEMS // over, min(s + 1, over) * ITEMS // over)

        raw_qkv = y[:, :, 0:3 * C]
        raw_w1 = xc[:, :, :]
        prf = pr[:, :, :, :].rearrange("p a b c -> p (a b c)")
        raw_w2 = prf[:, 0:HT * C].rearrange("p (t c) -> p t c", c=C)
        raw_proj = prf[:, 2048:2048 + CT * C].rearrange("p (t c) -> p t c", c=C)
        raw_fgh = prf[:, 2560:2560 + CT * 3 * DH].rearrange("p (t c) -> p t c", c=3 * DH)
        raw_wv = prf[0:3 * DH, 2816:2816 + C]
        scaled_wv = prf[0:3 * DH, 3072:3072 + C]

        block = ctx.enter_context(nc.Block())

        @block.sync
        def _(sp):
            def load_x(img):
                sp.dma_start(xin[:, :, :], x[bass.ds(img, 1), :, :].rearrange("a (t p) n -> p (a t) n", p=P)
                             ).then_inc(x_loaded, DMA)

            sp.dma_start(vec[:, :], vecs).then_inc(vec_loaded, DMA)
            for t in range(CT):
                rows = slice(t * P, t * P + P)
                sp.dma_start(raw_qkv[:, t, :], wqkv[rows, :]).then_inc(weights_loaded, DMA)
                sp.dma_start(raw_w1[:, t, :], w1[rows, :]).then_inc(weights_loaded, DMA)
                sp.dma_start(raw_proj[:, t, :], wproj[rows, :]).then_inc(weights_loaded, DMA)
                sp.dma_start(raw_fgh[:, t, :], wfgh[rows, :]).then_inc(weights_loaded, DMA)
            sp.dma_start(raw_w2, w2.rearrange("(t p) c -> p t c", p=P)).then_inc(weights_loaded, DMA)
            for r in range(3):
                sp.dma_start(raw_wv[r * DH:r * DH + DH, :], wv).then_inc(weights_loaded, DMA)
            load_x(0)
            sp.sem_inc(y_free, 1)

            def image(img, more):
                for g in range(GROUPS):
                    for half, dst, placed, parts in ((0, qs, q_stacked, (0, 1, 0)), (1, ks, k_stacked, (2, 2, 3))):
                        sp.wait_ge(qk_staged, img * 2 * GROUPS + 2 * g + half + 1)
                        for j in range(G):
                            for r, part in enumerate(parts):
                                sp.dma_start(dst[r * DH:r * DH + DH, G * g + j, :].bitcast(F32),
                                             stage[j * DH:j * DH + DH, part, :].bitcast(F32)).then_inc(placed, DMA)
                    if g == 0:
                        place_negm(img, 0)
                place_negm(img, 1)
                sp.wait_ge(y_ready, img * CT + CT)
                if more:
                    load_x(img + 1)
                place_negm(img, 2)
                for t in range(CT):
                    sp.wait_ge(out_ready, img * CT + t + 1)
                    sp.dma_start(out[bass.ds(img, 1), t * P:t * P + P, :].rearrange("a p n -> p (a n)"),
                                 y[:, t, :]).then_inc(y_free, DMA)

            def place_negm(img, k):
                n = ITEMS if k < 2 else KT
                sp.wait_ge(max_read, img * MAXES + (ITEMS * NCH + 1) * k + n * NCH + 1)
                first = G * k if k < 2 else 0
                sp.dma_start(qs[NEG:NEG + 1, first:first + n // KT, :].bitcast(F32).rearrange("p a (b c) -> p (a b) c", c=P),
                             negm[0:n, :].bitcast(F32)).then_inc(negm_placed, DMA)

            with sp.Fori(0, IMGS - 1) as img:
                image(img, True)
            image(IMGS - 1, False)
            sp.wait_ge(y_free, 1 + IMGS * CT * DMA)

        @block.gpsimd
        def _(pool):
            nc.gpsimd.memset(avg[:, :], 1.0 / C).then_inc(consts_ready, 1)
            nc.gpsimd.memset(ones[:, :], 1.0).then_inc(consts_ready, 1)
            nc.gpsimd.memset(eps[:, :], EPS).then_inc(consts_ready, 1)
            pool.wait_ge(consts_ready, 3)
            nc.gpsimd.memset(ks[NEG:NEG + 1, :, :].bitcast(F32), 1.0).then_inc(consts_ready, 1)
            pool.wait_ge(consts_ready, 4)
            nc.gpsimd.memset(ident[:, :], 0.0).then_inc(consts_zeroed, 1)
            pool.wait_ge(consts_zeroed, 1)
            nc.gpsimd.affine_select(out=ident[:, :], in_=ident[:, :], compare_op=ALU.not_equal, fill=1.0, base=0,
                                    pattern=[[-1, P]], channel_multiplier=1).then_inc(consts_ready, 1)

        @block.tensor
        def _(pe):
            pe.wait_ge(vec_loaded, DMA)
            pe.wait_ge(weights_loaded, 12 * DMA)
            pe.wait_ge(consts_ready, 5)
            for o in range(3 * CT):
                for t in range(CT):
                    pe.matmul(maxp[:, 0, o:o + 1], raw_qkv[:, t, o * P:o * P + P],
                              vec[:, V_BETA1 + t:V_BETA1 + t + 1], start=t == 0, stop=t == CT - 1)
            for o in range(HT):
                for t in range(CT):
                    pe.matmul(maxp[:, 0, B_FFN + o:B_FFN + o + 1], raw_w1[:, t, o * P:o * P + P],
                              vec[:, V_BETA2 + t:V_BETA2 + t + 1], start=t == 0, stop=t == CT - 1)
            for o in range(CT):
                last = pe.matmul(maxp[:, 0, B_OUT + o:B_OUT + o + 1], raw_wv[0:DH, o * P:o * P + P],
                                 vec[0:DH, V_BH:V_BH + 1], start=True, stop=True)
            last.then_inc(bias_sums, 1)
            pe.wait_ge(bias_ready, 1)
            for o in range(CT):
                for t in range(CT):
                    last = pe.matmul(maxp[:, 1, o:o + 1], raw_proj[:, t, o * P:o * P + P],
                                     bias[:, B_V + t:B_V + t + 1], start=t == 0, stop=t == CT - 1)
            last.then_inc(bias_sums, 1)
            pe.wait_ge(weights_ready, 1)

            def stats(img, name, src):
                for n in range(NCH):
                    for t in range(CT):
                        last = pe.matmul(pair(name)[:, n, :], avg[:, :], src[:, t, n * CH:n * CH + CH],
                                         start=t == 0, stop=t == CT - 1)
                last.then_inc(job_ready, 1)

            def triple(dst, w, cols, src, tok, tiles):
                n_mm = 0
                for t in tiles:
                    for a, b in ((HI, HI), (LO, HI), (HI, LO)):
                        last = pe.matmul(dst, w[:, a, t, cols], src(b, t)[:, tok],
                                         start=n_mm == 0, stop=n_mm == 3 * len(tiles) - 1)
                        n_mm += 1
                return last

            def act_of(b, t):
                return act[:, b, t, :]

            def projection(img, name, w, cols):
                m = cols.stop - cols.start
                for n in range(NCH):
                    last = triple(pair(name)[0:m, n, :], w, cols, act_of, slice(n * CH, n * CH + CH), range(CT))
                last.then_inc(job_ready, 1)

            def values(img, half):
                name = f"vals{half}"
                for i in range(4):
                    k = 4 * half + i
                    dst = pair(name)[:, i // 2, (i % 2) * C:(i % 2) * C + C]
                    n_mm = 0
                    for t in range(CT):
                        for a, b in ((HI, HI), (LO, HI), (HI, LO)):
                            last = pe.matmul(dst, act[:, a, t, k * P:k * P + P], wqkv_s[:, b, t, 2 * C:3 * C],
                                             start=n_mm == 0, stop=n_mm == 3 * CT - 1)
                            n_mm += 1
                last.then_inc(job_ready, 1)

            def max_use(img, idx):
                if idx >= 2:
                    pe.wait_ge(max_read, img * MAXES + idx - 1)
                return maxp[:, idx % 2, :]

            def max_pass(img, grp, items):
                for it in items:
                    h = G * grp + it // KT if grp < 2 else 0
                    t = it % KT
                    for n in range(NCH):
                        idx = (ITEMS * NCH + 1) * grp + it * NCH + n
                        pe.matmul(max_use(img, idx), qs[0:NEG, h, t * P:t * P + P],
                                  ks[0:NEG, h, n * CH:n * CH + CH], start=True, stop=True).then_inc(max_scores, 1)

            def max_turn(img, grp):
                n = ITEMS if grp < 2 else KT
                idx = (ITEMS * NCH + 1) * grp + n * NCH
                bank = max_use(img, idx)
                pe.wait_ge(max_ready, img * 3 + grp + 1)
                pe.transpose(bank[0:n, 0:P], mxc[:, 0:n], ident[:, :]).then_inc(max_scores, 1)

            def half_scores(img, idx, cols):
                if idx >= 2:
                    pe.wait_ge(exp_done, img * HALVES + idx - 1)
                for i, (h, kt, n) in enumerate(cols):
                    last = pe.matmul(lin[:, idx % 2, i, :], ks[0:NEG + 1, h, kt * P:kt * P + P],
                                     qs[0:NEG + 1, h, n * CH:n * CH + CH], start=True, stop=True)
                last.then_inc(scores_ready, 1)

            def step_scores(img, g, s):
                n, kt = s // KT, s % KT
                for p in range(2):
                    half_scores(img, (g * STEPS + s) * 2 + p, [(G * g + 2 * p + i, kt, n) for i in range(2)])

            def step_pv(img, g, s):
                n, kt = s // KT, s % KT
                idx = (g * STEPS + s) * 2
                pe.wait_ge(exp_done, img * HALVES + idx + 2)
                if kt == 0 and g + n > 0:
                    pe.wait_ge(den_copied, img * 4 + 2 * g + n)
                    pe.wait_ge(num_copied, img * 4 + 2 * g + n)
                for j in range(G):
                    pe.matmul(att_o[j * DH:j * DH + DH, :], vals[:, kt, (G * g + j) * DH:(G * g + j + 1) * DH],
                              pr[:, (idx + j // 2) % 4, j % 2, :], start=kt == 0, stop=kt == KT - 1)
                for j in range(G):
                    last = pe.matmul(att_d[j * DH:j * DH + DH, :], ones[:, :],
                                     pr[:, (idx + j // 2) % 4, j % 2, :], start=kt == 0, stop=kt == KT - 1)
                last.then_inc(pv_done, 1)

            def hidden_up(img, n, j):
                name = f"up{n}_{j}"
                for i in range(2):
                    m = 2 * j + i
                    last = triple(pair(name)[:, i, :], w1_s, slice(m * P, m * P + P), act_of,
                                  slice(n * CH, n * CH + CH), range(CT))
                last.then_inc(job_ready, 1)

            def hidden_down(img, n):
                name = f"down{n}"
                for k in range(HT):
                    if k % 2 == 0:
                        pe.wait_ge(hid_split, img * 2 * 4 + n * 4 + k // 2 + 1)
                    for m in range(CT):
                        for i, (a, b) in enumerate(((HI, hid_hi), (LO, hid_hi), (HI, hid_lo))):
                            last = pe.matmul(pair(name)[:, m, :], w2_s[:, a, k, m * P:m * P + P], b[:, k, :],
                                             start=k == 0 and i == 0, stop=k == HT - 1 and i == 2)
                last.then_inc(job_ready, 1)

            def image(img):
                pe.wait_ge(x_loaded, img * DMA + DMA)
                stats(img, "mean1", xin)
                pe.wait_ge(squared, img * 2 * CT + CT)
                stats(img, "var1", sq)
                pe.wait_ge(act_ready, img * 2 * CT + CT)
                projection(img, "q0", wqkv_s, slice(0, P))
                wait_freed(pe, img, "mean1")
                projection(img, "k0", wqkv_s, slice(C, C + P))
                wait_freed(pe, img, "var1")
                values(img, 0)
                wait_freed(pe, img, "q0")
                values(img, 1)
                wait_freed(pe, img, "k0")
                projection(img, "q1", wqkv_s, slice(P, C))
                wait_freed(pe, img, "vals0")
                projection(img, "k1", wqkv_s, slice(C + P, 2 * C))
                pe.wait_ge(q_stacked, (img * GROUPS * G * 3 + G * 3) * DMA)
                pe.wait_ge(k_stacked, (img * GROUPS * G * 3 + G * 3) * DMA)
                max_pass(img, 0, range(ITEMS))
                max_turn(img, 0)

                wait_freed(pe, img, "vals1")
                wait_freed(pe, img, "k1")
                for g in range(GROUPS):
                    pe.wait_ge(negm_placed, (img * 3 + g + 1) * DMA)
                    if g == 0:
                        pe.wait_ge(q_stacked, (img + 1) * GROUPS * G * 3 * DMA)
                        pe.wait_ge(k_stacked, (img + 1) * GROUPS * G * 3 * DMA)
                    for s in range(STEPS):
                        step_scores(img, g, s)
                        if g == 0:
                            max_pass(img, 1, items_of(s))
                            if s == STEPS - 2:
                                max_turn(img, 1)
                        if s > 0:
                            step_pv(img, g, s - 1)
                    step_pv(img, g, STEPS - 1)

                for g in range(GROUPS):
                    pe.wait_ge(heads_ready, img * 4 + 2 * g + 2)
                projection(img, "proj0", wproj_s, slice(0, P))
                pe.wait_ge(exp_done, img * HALVES + L0_HALVES)
                projection(img, "proj1", wproj_s, slice(P, C))
                pe.wait_ge(y_ready, img * CT + CT)
                stats(img, "mean2", y)
                wait_freed(pe, img, "proj0")
                pe.wait_ge(squared, img * 2 * CT + 2 * CT)
                stats(img, "var2", sq)
                pe.wait_ge(act_ready, img * 2 * CT + 2 * CT)
                for n in range(NCH):
                    for j in range(4):
                        wait_freed(pe, img, JOBS[JOB[f"up{n}_{j}"] - 3])
                        hidden_up(img, n, j)
                    wait_freed(pe, img, f"up{n}_1")
                    hidden_down(img, n)

                wait_freed(pe, img, "up1_2")
                pe.wait_ge(y2_split, img * NCH + NCH)
                projection(img, "f", wfg_s, slice(0, 3 * DH))
                wait_freed(pe, img, "up1_3")
                projection(img, "g", wfg_s, slice(3 * DH, 6 * DH))
                wait_freed(pe, img, "down1")
                for k in range(KT):
                    n_mm = 0
                    for t in range(CT):
                        for a, b in ((HI, HI), (LO, HI), (HI, LO)):
                            last = pe.matmul(pair("h")[:, 0, k * DH:k * DH + DH], act[:, a, t, k * P:k * P + P],
                                             wh_s[:, b, t, :], start=n_mm == 0, stop=n_mm == 3 * CT - 1)
                            n_mm += 1
                last.then_inc(job_ready, 1)
                pe.wait_ge(fg_stacked, img * 2 + 2)
                max_pass(img, 2, range(KT))
                max_turn(img, 2)
                wait_freed(pe, img, "h")
                pe.wait_ge(negm_placed, (img * 3 + 3) * DMA)
                for kt in range(KT + 1):
                    if kt < KT:
                        half_scores(img, L0_HALVES + kt, [(0, kt, n) for n in range(NCH)])
                    if kt > 0:
                        k = kt - 1
                        idx = L0_HALVES + k
                        pe.wait_ge(exp_done, img * HALVES + idx + 1)
                        for n in range(NCH):
                            pe.matmul(att_o[n * DH:n * DH + DH, :], vals1[:, k, :], pr[:, idx % 4, n, :],
                                      start=k == 0, stop=k == KT - 1)
                        for n in range(NCH):
                            last = pe.matmul(att_o[2 * DH + n * DH:3 * DH + n * DH, :], ones[:, :], pr[:, idx % 4, n, :],
                                             start=k == 0, stop=k == KT - 1)
                        last.then_inc(pv_done, 1)
                pe.wait_ge(x0_split, img + 1)
                for m in range(CT):
                    for n in range(NCH):
                        last = pe.matmul(pair(f"out{m}")[:, n, :], wv_s[:, m * P:m * P + P],
                                         x0s[:, n * CH:n * CH + CH], start=True, stop=True)
                    last.then_inc(job_ready, 1)
                wait_freed(pe, img, "out1")
                pe.wait_ge(max_read, (img + 1) * MAXES)

            with pe.Fori(0, IMGS) as img:
                image(img)

        @block.scalar
        def _(sc):
            sc.preload_act_table_set("natural_log_exp_and_others")
            sc.wait_ge(weights_ready, 1)
            sc.wait_ge(consts_ready, 5)

            def norm(img, which):
                for t in range(CT):
                    sc.wait_ge(centred, img * 2 * CT + which * CT + t + 1)
                    nc.scalar.activation(sq[:, t, :], xc[:, t, :], ACT.Square).then_inc(squared, 1)
                sc.wait_ge(job_ready, job_done(img, f"var{which + 1}"))
                nc.scalar.activation(sq[:, 0, :], pair(f"var{which + 1}"), ACT.Ln, bias=eps[:, 0:1]).then_inc(log_ready, 1)
                sc.wait_ge(log_ready, img * 2 + which + 1)
                nc.scalar.activation(sq[:, 1, :], sq[:, 0, :], ACT.Exp, scale=-0.5).then_inc(guess_ready, 1)
                for t in range(CT):
                    sc.wait_ge(normed, img * 2 * CT + which * CT + t + 1)
                    nc.scalar.copy(act[:, HI, t, :], xc[:, t, :]).then_inc(normed_hi, 1)

            def qk_evac(img, name, slot, col):
                sc.wait_ge(job_ready, job_done(img, name))
                nc.scalar.activation(stage[:, slot, :], pair(name), ACT.Identity,
                                     bias=bias[:, col:col + 1]).then_inc(qk_hi, 1)

            def vals_evac(img, half):
                sc.wait_ge(job_ready, job_done(img, f"vals{half}"))
                nc.scalar.copy(vals[:, 4 * half:4 * half + 4, :], pair(f"vals{half}")).then_inc(vals_ready, 1)

            def half_exp(img, idx, scale):
                sc.wait_ge(scores_ready, img * HALVES + idx + 1)
                if 4 <= idx < L0_HALVES:
                    sc.wait_ge(pv_done, img * PV + (idx - 4) // 2 + 1)
                elif idx >= L0_HALVES + 4:
                    sc.wait_ge(pv_done, img * PV + GROUPS * STEPS + idx - 4 - L0_HALVES + 1)
                elif idx >= L0_HALVES:
                    sc.wait_ge(pv_done, img * PV + GROUPS * STEPS)
                nc.scalar.activation(pr[:, idx % 4, :, :], lin[:, idx % 2, :, :], ACT.Exp,
                                     scale=scale).then_inc(exp_done, 1)

            def den_copy(img, g, n):
                sc.wait_ge(pv_done, img * PV + (g * NCH + n + 1) * KT)
                if g + n > 0:
                    sc.wait_ge(quot_ready, img * 4 + 2 * g + n)
                nc.scalar.copy(den, att_d).then_inc(den_copied, 1)

            def quot_split(img, g, n):
                sc.wait_ge(quot_ready, img * 4 + 2 * g + n + 1)
                nc.scalar.copy(act[:, HI, g, n * CH:n * CH + CH], quot).then_inc(quot_hi, 1)

            def image(img):
                norm(img, 0)
                qk_evac(img, "q0", 0, B_QK)
                qk_evac(img, "k0", 2, B_QK + 2)
                vals_evac(img, 0)
                vals_evac(img, 1)
                sc.wait_ge(q_stacked, (img * GROUPS + 1) * G * 3 * DMA)
                qk_evac(img, "q1", 0, B_QK + 1)
                sc.wait_ge(k_stacked, (img * GROUPS + 1) * G * 3 * DMA)
                qk_evac(img, "k1", 2, B_QK + 3)
                for g in range(GROUPS):
                    for s in range(STEPS):
                        for p in range(2):
                            half_exp(img, (g * STEPS + s) * 2 + p, SCALE)
                        if s == 0 and g > 0:
                            den_copy(img, g - 1, 1)
                        if s == 6 and g > 0:
                            quot_split(img, g - 1, 1)
                        if s == KT:
                            den_copy(img, g, 0)
                        if s == STEPS - 2:
                            quot_split(img, g, 0)
                den_copy(img, 1, 1)
                quot_split(img, 1, 1)
                norm(img, 1)
                for n in range(NCH):
                    for j in range(4):
                        i = n * 4 + j
                        sc.wait_ge(job_ready, job_done(img, f"up{n}_{j}"))
                        if i >= 2:
                            sc.wait_ge(hid_split, img * 8 + i - 1)
                        for e in range(2):
                            nc.scalar.activation(hid32[:, j % 2, e * CH:e * CH + CH], pair(f"up{n}_{j}")[:, e, :],
                                                 ACT.Relu, bias=bias[:, B_FFN + 2 * j + e:B_FFN + 2 * j + e + 1]
                                                 ).then_inc(hid_ready, 1)
                        sc.wait_ge(hid_ready, img * 16 + 2 * i + 2)
                        if n == 1 and j == 0:
                            sc.wait_ge(job_ready, job_done(img, "down0"))
                        nc.scalar.copy(hid_hi[:, 2 * j:2 * j + 2, :],
                                       hid32[:, j % 2, :].rearrange("p (a c) -> p a c", c=CH)).then_inc(hid_hi_ready, 1)
                    if n == 1:
                        y2_split_hi(img, 0)
                y2_split_hi(img, 1)
                for i, (name, dst) in enumerate((("f", qs), ("g", ks))):
                    sc.wait_ge(job_ready, job_done(img, name))
                    nc.scalar.activation(dst[0:3 * DH, 0, :], pair(name)[0:3 * DH], ACT.Identity,
                                         bias=vec[0:3 * DH, V_BF + i:V_BF + i + 1]).then_inc(fg_hi, 1)
                sc.wait_ge(job_ready, job_done(img, "h"))
                nc.scalar.copy(vals1[:, :, :], pair("h")[:, 0, 0:KT * DH].rearrange("p (a c) -> p a c", c=DH)
                               ).then_inc(vals1_ready, 1)
                for kt in range(KT):
                    half_exp(img, L0_HALVES + kt, 1.0)
                sc.wait_ge(x0_ready, img * NCH + NCH)
                for r in (0, 2):
                    nc.scalar.copy(x0s[r * DH:r * DH + DH, :], x0).then_inc(x0_hi, 1)

            def y2_split_hi(img, n):
                sc.wait_ge(y2_ready, img * 2 * CT + CT * (n + 1))
                nc.scalar.copy(act[:, HI, :, n * CH:n * CH + CH], y[:, :, n * CH:n * CH + CH]).then_inc(y2_hi, 1)

            with sc.Fori(0, IMGS) as img:
                image(img)

        @block.vector
        def _(ve):
            V = nc.vector
            ve.wait_ge(vec_loaded, DMA)
            ve.wait_ge(weights_loaded, 12 * DMA)
            ve.wait_ge(bias_sums, 1)
            V.tensor_copy(bias[:, B_QK:B_V + CT], maxp[:, 0, B_QK:B_V + CT]).then_inc(bias_ready, 1)
            V.tensor_tensor(bias[:, B_FFN:B_FFN + HT], maxp[:, 0, B_FFN:B_FFN + HT], vec[:, V_B1:V_B1 + HT], ALU.add)
            V.tensor_tensor(bias[:, B_OUT:B_OUT + CT], maxp[:, 0, B_OUT:B_OUT + CT], vec[:, V_BV:V_BV + CT],
                            ALU.add).then_inc(split_step, 1)
            ve.wait_ge(split_step, 1)
            V.tensor_scalar(bias[:, B_OUT:B_OUT + CT], bias[:, B_OUT:B_OUT + CT], vec[:, V_GAMMA:V_GAMMA + 1], None,
                            ALU.mult)
            ve.wait_ge(bias_sums, 2)
            V.tensor_tensor(bias[:, B_PROJ:B_PROJ + CT], maxp[:, 1, 0:CT], vec[:, V_BPROJ:V_BPROJ + CT], ALU.add)
            steps = 1
            for raw, dst, gain in ((raw_qkv, wqkv_s, V_G1), (raw_w1, w1_s, V_G2)):
                for t in range(CT):
                    V.tensor_scalar(raw[:, t, :], raw[:, t, :], vec[:, gain + t:gain + t + 1], None,
                                    ALU.mult).then_inc(split_step, 1)
                steps += CT
            V.tensor_scalar(scaled_wv, raw_wv, vec[0:3 * DH, V_GAMMA:V_GAMMA + 1], None, ALU.mult).then_inc(split_step, 1)
            steps += 1
            ve.wait_ge(split_step, steps)
            splits = [(raw_qkv, wqkv_s[:, :, :, :]), (raw_w1, w1_s[:, :, :, :]), (raw_w2, w2_s[:, :, :, :]),
                      (raw_proj, wproj_s[:, :, :, :]), (raw_fgh[:, :, 2 * DH:3 * DH], wh_s[:, :, :, :])]
            splits += [(raw_fgh[:, :, i * DH:i * DH + DH], wfg_s[:, :, :, (3 * i + r) * DH:(3 * i + r + 1) * DH])
                       for i in range(2) for r in range(3)]
            for raw, dst in splits:
                V.tensor_copy(dst[:, HI], raw).then_inc(split_step, 1)
            V.tensor_copy(wv_s[:, :], scaled_wv).then_inc(split_step, 1)
            steps += len(splits) + 1
            ve.wait_ge(split_step, steps)
            for raw, dst in splits:
                V.tensor_tensor(dst[:, LO], raw, dst[:, HI].bitcast(F32), ALU.subtract)
            V.tensor_tensor(wv_s[2 * DH:3 * DH, :], scaled_wv[2 * DH:3 * DH, :], wv_s[2 * DH:3 * DH, :].bitcast(F32),
                            ALU.subtract).then_inc(weights_ready, 1)

            def norm(img, which, src):
                mean, var = f"mean{which + 1}", f"var{which + 1}"
                ve.wait_ge(job_ready, job_done(img, mean))
                for t in range(CT):
                    last = V.tensor_tensor(xc[:, t, :], src[:, t, :],
                                           pair(mean).rearrange("p a b -> p (a b)"), ALU.subtract)
                    last.then_inc(centred, 1)
                ve.wait_ge(centred, img * 2 * CT + which * CT + CT)
                ve.wait_ge(guess_ready, img * 2 + which + 1)
                base = img * 6 + which * 3
                V.tensor_tensor(sq[:, 0, :], sq[:, 1, :], sq[:, 1, :], ALU.mult).then_inc(newton, 1)
                ve.wait_ge(newton, base + 1)
                V.scalar_tensor_tensor(out=sq[:, 0, :], in0=pair(var).rearrange("p a b -> p (a b)"), scalar=EPS,
                                       in1=sq[:, 0, :], op0=ALU.add, op1=ALU.mult).then_inc(newton, 1)
                ve.wait_ge(newton, base + 2)
                V.tensor_scalar(sq[:, 0, :], sq[:, 0, :], -0.5, 1.5, ALU.mult, ALU.add).then_inc(newton, 1)
                ve.wait_ge(newton, base + 3)
                V.tensor_tensor(sq[:, 0, :], sq[:, 0, :], sq[:, 1, :], ALU.mult).then_inc(rstd_ready, 1)
                ve.wait_ge(rstd_ready, img * 2 + which + 1)
                for t in range(CT):
                    V.tensor_tensor(xc[:, t, :], xc[:, t, :], sq[:, 0, :], ALU.mult).then_inc(normed, 1)
                for t in range(CT):
                    ve.wait_ge(normed_hi, img * 2 * CT + which * CT + t + 1)
                    V.tensor_tensor(act[:, LO, t, :], xc[:, t, :], act[:, HI, t, :].bitcast(F32),
                                    ALU.subtract).then_inc(act_ready, 1)

            def qk_lo(img, k, name, slot, col):
                ve.wait_ge(qk_hi, img * 4 + k + 1)
                V.scalar_tensor_tensor(out=stage[:, slot + 1, :], in0=pair(name).rearrange("p a b -> p (a b)"),
                                       scalar=bias[:, col:col + 1], in1=stage[:, slot, :].bitcast(F32),
                                       op0=ALU.add, op1=ALU.subtract).then_inc(qk_staged, 1)

            def max_reduce(img, grp, items):
                for it in items:
                    for n in range(NCH):
                        idx = (ITEMS * NCH + 1) * grp + it * NCH + n
                        ve.wait_ge(max_scores, img * MAXES + idx + 1)
                        V.tensor_reduce(mx[:, n, it:it + 1], maxp[:, idx % 2, :], AX.X, ALU.max).then_inc(max_read, 1)

            def max_combine(img, grp):
                n = ITEMS if grp < 2 else KT
                idx = (ITEMS * NCH + 1) * grp + n * NCH
                ve.wait_ge(max_read, img * MAXES + idx)
                V.tensor_tensor(mxc[:, 0:n], mx[:, 0, 0:n], mx[:, 1, 0:n], ALU.max).then_inc(max_ready, 1)

            def max_negate(img, grp):
                n = ITEMS if grp < 2 else KT
                idx = (ITEMS * NCH + 1) * grp + n * NCH
                ve.wait_ge(max_scores, img * MAXES + idx + 1)
                V.tensor_scalar(negm[0:n, :], maxp[0:n, idx % 2, 0:P], -1.0, None, ALU.mult).then_inc(max_read, 1)

            def num_copy(img, g, n):
                ve.wait_ge(pv_done, img * PV + (g * NCH + n + 1) * KT)
                if g + n > 0:
                    ve.wait_ge(heads_ready, img * 4 + 2 * g + n)
                V.tensor_copy(quot, att_o).then_inc(num_copied, 1)

            def recip(img, g, n, parts):
                k = img * 4 + 2 * g + n
                ve.wait_ge(den_copied, k + 1)
                for q in parts:
                    V.reciprocal(den[:, q * P:q * P + P], den[:, q * P:q * P + P]).then_inc(recip_ready, 1)

            def quotient(img, g, n):
                k = img * 4 + 2 * g + n
                ve.wait_ge(recip_ready, 4 * k + 4)
                ve.wait_ge(num_copied, k + 1)
                V.tensor_tensor(quot, quot, den, ALU.mult).then_inc(quot_ready, 1)

            def quotient_lo(img, g, n):
                ve.wait_ge(quot_hi, img * 4 + 2 * g + n + 1)
                V.tensor_tensor(act[:, LO, g, n * CH:n * CH + CH], quot, act[:, HI, g, n * CH:n * CH + CH].bitcast(F32),
                                ALU.subtract).then_inc(heads_ready, 1)

            def quotient_steps(img, g, n, at):
                if at == 0:
                    num_copy(img, g, n)
                elif at <= 4:
                    recip(img, g, n, [at - 1])
                elif at == 5:
                    quotient(img, g, n)
                elif at == 7:
                    quotient_lo(img, g, n)

            def image(img):
                norm(img, 0, xin)
                qk_lo(img, 0, "q0", 0, B_QK)
                qk_lo(img, 1, "k0", 2, B_QK + 2)
                qk_lo(img, 2, "q1", 0, B_QK + 1)
                qk_lo(img, 3, "k1", 2, B_QK + 3)
                max_reduce(img, 0, range(ITEMS))
                max_combine(img, 0)
                max_negate(img, 0)
                for g in range(GROUPS):
                    for s in range(STEPS):
                        if g == 0:
                            max_reduce(img, 1, items_of(s))
                            if s == STEPS - 3:
                                max_combine(img, 1)
                            if s == STEPS - 2:
                                max_negate(img, 1)
                        if s < KT and g > 0:
                            quotient_steps(img, g - 1, 1, s)
                        elif s >= KT:
                            quotient_steps(img, g, 0, s - KT)
                num_copy(img, 1, 1)
                recip(img, 1, 1, range(4))
                quotient(img, 1, 1)
                quotient_lo(img, 1, 1)

                ve.wait_ge(y_free, img * CT * DMA + 1)
                for m in range(CT):
                    ve.wait_ge(job_ready, job_done(img, f"proj{m}"))
                    V.scalar_tensor_tensor(out=y[:, m, :], in0=pair(f"proj{m}").rearrange("p a b -> p (a b)"),
                                           scalar=bias[:, B_PROJ + m:B_PROJ + m + 1], in1=xin[:, m, :],
                                           op0=ALU.add, op1=ALU.add).then_inc(y_ready, 1)
                ve.wait_ge(y_ready, img * CT + CT)
                norm(img, 1, y)
                for n in range(NCH):
                    chunk = slice(n * CH, n * CH + CH)
                    for j in range(4):
                        ve.wait_ge(hid_hi_ready, img * 8 + 4 * n + j + 1)
                        V.tensor_tensor(hid_lo[:, 2 * j:2 * j + 2, :],
                                        hid32[:, j % 2, :].rearrange("p (a c) -> p a c", c=CH),
                                        hid_hi[:, 2 * j:2 * j + 2, :].bitcast(F32), ALU.subtract).then_inc(hid_split, 1)
                    ve.wait_ge(job_ready, job_done(img, f"down{n}"))
                    for m in range(CT):
                        V.scalar_tensor_tensor(out=y[:, m, chunk], in0=pair(f"down{n}")[:, m, :],
                                               scalar=vec[:, V_B2 + m:V_B2 + m + 1], in1=y[:, m, chunk],
                                               op0=ALU.add, op1=ALU.add).then_inc(y2_ready, 1)
                for n in range(NCH):
                    chunk = slice(n * CH, n * CH + CH)
                    ve.wait_ge(y2_hi, img * NCH + n + 1)
                    V.tensor_tensor(act[:, LO, :, chunk], y[:, :, chunk], act[:, HI, :, chunk].bitcast(F32),
                                    ALU.subtract).then_inc(y2_split, 1)

                for i, (name, dst, row, col) in enumerate((("f", qs, 1, V_BF), ("g", ks, 2, V_BG))):
                    ve.wait_ge(fg_hi, img * 2 + i + 1)
                    rows = slice(row * DH, row * DH + DH)
                    V.scalar_tensor_tensor(out=dst[rows, 0, :], in0=pair(name)[rows].rearrange("p a b -> p (a b)"),
                                           scalar=vec[rows, col:col + 1], in1=dst[rows, 0, :].bitcast(F32),
                                           op0=ALU.add, op1=ALU.subtract).then_inc(fg_stacked, 1)
                max_reduce(img, 2, range(KT))
                max_combine(img, 2)
                max_negate(img, 2)
                ve.wait_ge(pv_done, img * PV + PV)
                V.reciprocal(sq[0:2 * DH, 0, 0:CH], att_o[2 * DH:4 * DH, :]).then_inc(x0_recip, 1)
                ve.wait_ge(x0_recip, img + 1)
                for n in range(NCH):
                    rows = slice(n * DH, n * DH + DH)
                    V.tensor_tensor(x0[:, n * CH:n * CH + CH], att_o[rows, :], sq[rows, 0, 0:CH],
                                    ALU.mult).then_inc(x0_ready, 1)
                ve.wait_ge(x0_hi, img * 2 + 2)
                V.tensor_tensor(x0s[DH:2 * DH, :], x0, x0s[0:DH, :].bitcast(F32), ALU.subtract).then_inc(x0_split, 1)
                for m in range(CT):
                    ve.wait_ge(job_ready, job_done(img, f"out{m}"))
                    V.scalar_tensor_tensor(out=y[:, m, :], in0=pair(f"out{m}").rearrange("p a b -> p (a b)"),
                                           scalar=bias[:, B_OUT + m:B_OUT + m + 1], in1=y[:, m, :],
                                           op0=ALU.add, op1=ALU.add).then_inc(out_ready, 1)

            ve.wait_ge(weights_ready, 1)
            with ve.Fori(0, IMGS) as img:
                image(img)


def kernel(**inputs):
    import concourse.bacc as bacc
    import numpy as np
    from concourse.bass_utils import run_bass_kernel_spmd

    a = {k: np.asarray(v) for k, v in inputs.items()}
    x = np.ascontiguousarray(a["x"])
    imgs, c, hh, ww = x.shape

    def columns(v):
        v = np.tile(v, P // v.size) if v.size < P else v
        return v.reshape(-1, P).T

    vecs = np.concatenate([columns(a[n]) for n in (
        "L0_conv_g1", "L0_conv_beta1", "L0_conv_g2", "L0_conv_beta2", "L0_conv_b_proj", "L0_conv_b1", "L0_conv_b2",
        "L1_conv_bv", "L1_conv_bf", "L1_conv_bg", "L1_conv_bh", "L1_conv_gamma")], axis=1)
    arrays = {
        "x": x.reshape(imgs, c, hh * ww),
        "wqkv": a["L0_conv_w_qkv"].T,
        "wproj": a["L0_conv_w_proj"].T,
        "w1": a["L0_conv_w1"].T,
        "w2": a["L0_conv_w2"].T,
        "wfgh": np.concatenate([a["L1_conv_wf"], a["L1_conv_wg"], a["L1_conv_wh"]], axis=0).T,
        "wv": a["L1_conv_wv"].T,
        "vecs": vecs,
    }
    arrays = {f"in_{k}": np.ascontiguousarray(v) for k, v in arrays.items()}
    nc = bacc.Bacc("TRN2", target_bir_lowering=False, num_devices=1)
    args = [nc.dram_tensor(k, v.shape, F32, kind="ExternalInput").ap() for k, v in arrays.items()]
    args.append(nc.dram_tensor("out_y", (imgs, c, hh * ww), F32, kind="ExternalOutput").ap())
    attention_layers(nc, *args)
    r = run_bass_kernel_spmd(nc, [arrays], core_ids=[0])
    return r.results[0]["out_y"].reshape(x.shape)
```

```python
from contextlib import ExitStack

import concourse.bass as bass
from concourse import mybir

F32 = mybir.dt.float32
F32R = mybir.dt.float32r
ALU = mybir.AluOpType
ACT = mybir.ActivationFunctionType
AX = mybir.AxisListType

P = 128
DH = 32
HI, LO = 0, 1
NEG = 3 * DH
CH = 512
EPS = 1e-5
DMA = 16

V_G1, V_BETA1, V_G2, V_BETA2, V_BPROJ, V_B1, V_B2, V_BV, V_BF, V_BG, V_BH, V_GAMMA, V_COLS = (
    0, 2, 4, 6, 8, 10, 18, 20, 22, 23, 24, 25, 26)
B_QK, B_V, B_PROJ, B_FFN, B_OUT, B_COLS = 0, 4, 6, 8, 16, 18


def attention_layers(nc, x, wqkv, wproj, w1, w2, wfgh, wv, vecs, out):
    IMGS, C, N = x.shape
    CT = C // P
    KT = N // P
    NCH = N // CH
    HEADS = C // DH
    G = P // DH
    GROUPS = HEADS // G
    HID = w1.shape[1]
    HT = HID // P
    SCALE = float(DH) ** -0.5
    assert (CT, KT, NCH, G, GROUPS, HT) == (2, 8, 2, 4, 2, 8)

def split_evenly(n, parts, i):
    return range(n * i // parts, n * (i + 1) // parts)


class Plan:

    def __init__(self, jobs, segments, places, more=True, previous=True, jobs_before=0, uses_before=0, places_before=0):
        self.jobs, self.segments, self.places = jobs, segments, places
        self.uses = [use for part in segments.values() for use in part]
        self.more, self.previous = more, previous
        self.jobs_before, self.uses_before, self.places_before = jobs_before, uses_before, places_before


def attention_layers(nc, x, wqkv, wproj, w1, w2, wfgh, wv, vecs, out):
    IMGS, C, N = x.shape
    CT = C // P
    KT = N // P
    NCH = N // CH
    HEADS = C // DH
    G = P // DH
    GROUPS = HEADS // G
    HID = w1.shape[1]
    HT = HID // P
    SCALE = float(DH) ** -0.5
    assert (CT, KT, NCH, G, GROUPS, HT) == (2, 8, 2, 4, 2, 8)

    STEPS = NCH * KT
    L0_HALVES = GROUPS * STEPS * 2
    HALVES = L0_HALVES + KT
    PV = GROUPS * STEPS + KT
    ITEMS = G * KT
    STACK = 6 * DMA

    NEXT = ("vals0", "vals1", "q1", "k1")
    LOOP_JOBS = (["vals0", "vals1"] + [f"up0_{j}" for j in range(4)] + ["down0"]
                 + [f"up1_{j}" for j in range(4)] + ["down1", "f", "g", "q1", "h", "k1"])
    PAIR = {name: i % 3 for i, name in enumerate(LOOP_JOBS)}
    NJ = len(LOOP_JOBS)

    def maxima(grp, items):
        return [("max", grp, it, n) for it in items for n in range(NCH)]

    HEAD_ORDER = [1, 2, 3, 0]
    SPREAD = {1: (3, 4, 5, 4, 3, 3, 5, 4, 4, 4, 5, 5, 5, 5, 5, 0), 0: (0, 0, 4, 5, 5, 5, 5, 5, 4, 3, 5, 4, 3, 4, 3, 3)}
    QK0 = [("q0", 0), ("k0", 0), ("q0", 1), ("k0", 1)]
    PREVIOUS = {0: [("x0 reciprocal", n, 0) for n in range(NCH)], 1: [("x0", n, 0) for n in range(NCH)],
                3: [("x0 lo", 0, 0)]}
    OUT = [("out", m, n) for m in range(CT) for n in range(NCH)]
    NEXT_NORM = {5: [("scale", 0, 0, 0), ("scale", 0, 0, 1)], 6: [("scale", 0, 0, 2), ("scale", 0, 0, 3)],
                 7: [("scale", 0, 0, 4)], 8: [("lo", 0, 0)],
                 10: [("scale", 0, 1, 0), ("scale", 0, 1, 1)], 11: [("scale", 0, 1, 2), ("scale", 0, 1, 3)],
                 12: [("scale", 0, 1, 4)], 13: [("lo", 0, 1)]}
    QUOTIENTS = {8: [("numerators", 0, 0)], 10: [("quotient", 0, 0, 0)], 11: [("quotient", 0, 0, 1)],
                 12: [("quotient", 0, 0, 2)], 13: [("heads", 0, 0)],
                 16: [("numerators", 0, 1)], 18: [("quotient", 0, 1, 0), ("quotient", 0, 1, 1)],
                 19: [("quotient", 0, 1, 2)], 20: [("heads", 0, 1)],
                 24: [("numerators", 1, 0)], 25: [("quotient", 1, 0, i) for i in range(3)], 26: [("heads", 1, 0)],
                 31: [("scale", 1, 0, i) for i in range(3)]}

    def loop_segments(more, previous):
        maxima1 = maxima(1, [j * KT + t for j in HEAD_ORDER for t in range(KT)])
        maxima0 = maxima(0, range(ITEMS))
        segments = {}
        for s in range(STEPS):
            segments[s] = [maxima1.pop(0) for _ in range(SPREAD[1][s])]
            if s == STEPS - 1:
                segments[s].append(("turn", 1))
            if previous:
                segments[s] += {4: OUT[:CT], 5: OUT[CT:]}.get(s, [])
            if more:
                segments[s] = ({4: [("var", 0, 0)], 9: [("var", 0, 1)]}.get(s, []) + segments[s]
                               + {2: [("mean", 0, 0)], 6: [("mean", 0, 1)], 9: [QK0[0]], 12: [QK0[1]], 13: [QK0[2]],
                                  14: [QK0[3]]}.get(s, []))
        for s in range(STEPS):
            segments[STEPS + s] = [maxima0.pop(0) for _ in range(SPREAD[0][s])] if more else []
            segments[STEPS + s] += {11: [("proj", 0, m) for m in range(CT)], 12: [("mean", 1, 0)]}.get(s, [])
            if s == 14:
                segments[STEPS + s].insert(0, ("var", 1, 0))
        segments["turn"] = maxima0 + [("turn", 0)] if more else []
        segments["proj"] = [("proj", 1, m) for m in range(CT)]
        segments["mean2"] = [("mean", 1, 1)]
        segments["var2"] = [("var", 1, 1)]
        segments["layer1"] = maxima(2, range(KT))
        segments["turn1"] = [("turn", 2)]
        return segments

    FIRST = Plan(list(NEXT),
                 {"mean": [("mean", 0, 0)], "mean, var": [("var", 0, 0), ("mean", 0, 1)], "var": [("var", 0, 1)],
                  "qk": QK0, "maxima": maxima(0, range(ITEMS)) + [("turn", 0)]}, [0])
    before = dict(jobs_before=len(FIRST.jobs), places_before=len(FIRST.places))
    START = Plan(LOOP_JOBS, loop_segments(True, False), [1, 0, 2], previous=False, uses_before=len(FIRST.uses), **before)
    before.update(uses_before=len(FIRST.uses) - len(OUT))
    LOOP = Plan(LOOP_JOBS, loop_segments(True, True), [1, 0, 2], **before)
    LAST = Plan([j for j in LOOP_JOBS if j not in NEXT], loop_segments(False, True), [1, 2], more=False, **before)
    FINISH = Plan([], {"out": OUT}, [], uses_before=LAST.uses_before + len(LAST.uses) - len(LOOP.uses))

    def job_done(pl, it, name):
        return pl.jobs_before + it * NJ + pl.jobs.index(name) + 1

    def uses_up_to(pl, it, use):
        return pl.uses_before + it * len(LOOP.uses) + pl.uses.index(use) + 1

    def place_no(pl, it, grp):
        return pl.places_before + it * len(LOOP.places) + pl.places.index(grp) + 1

    def image_next(pl, it):
        return 0 if pl is FIRST else it + 1

    with ExitStack() as ctx:
        def sb(name, shape, dt=F32):
            return ctx.enter_context(nc.sbuf_tensor(name, shape, dt))

        def sem(name):
            return ctx.enter_context(nc.semaphore(name))

        wqkv_s = sb("wqkv_s", [P, 2, CT, 3 * C], F32R)
        wproj_s = sb("wproj_s", [P, 2, CT, C], F32R)
        w1_s = sb("w1_s", [P, 2, CT, HID], F32R)
        w2_s = sb("w2_s", [P, 2, HT, C], F32R)
        wfhg_s = sb("wfhg_s", [P, 2, CT, 7 * DH], F32R)
        wv_s = sb("wv_s", [3 * DH, C], F32R)
        vec = sb("vec", [P, V_COLS])
        bias = sb("bias", [P, B_COLS])
        avg = sb("avg", [P, P])
        ones = sb("ones", [P, DH])
        ident = sb("ident", [P, P])
        eps = sb("eps", [P, 1])
        xin = sb("xin", [P, CT, N])
        y = sb("y", [P, CT, N])
        xc = sb("xc", [P, CT, N])
        sq = sb("sq", [P, CT, N])
        nrm = sb("nrm", [P, 2, CT, N], F32R)
        act = sb("act", [P, 2, CT, N], F32R)
        qs = sb("qs", [P, HEADS, N], F32R)
        ks = sb("ks", [P, HEADS, N], F32R)
        vals = sb("vals", [P, KT, C])
        vals1 = sb("vals1", [P, KT, DH])
        pr = sb("pr", [P, 4, 2, CH])
        mx = sb("mx", [P, NCH, ITEMS])
        mxc = sb("mxc", [P, ITEMS])
        negm = sb("negm", [ITEMS, P], F32R)
        hid_hi = ks[:, G:2 * G, :].rearrange("p a (b c) -> p (a b) c", c=CH)
        hid_lo = qs[:, G:2 * G, :].rearrange("p a (b c) -> p (a b) c", c=CH)
        q0_stage, k0_stage = xc[:, :, :].bitcast(F32R), y[:, :, :].bitcast(F32R)
        stage1 = act[:, :, :, :].rearrange("p a t n -> p (a t) n")
        f_stack, g_stack = qs[:, G, :], ks[:, G, :]
        x0s = qs[0:3 * DH, G, :]
        den = sq[:, 0, 0:CH]
        quot = sq[:, 1, 0:CH]

        def guess(g, n):
            return y[:, 0, 0:CH] if g + n == 0 else sq[:, 0, CH:2 * CH]

        att_copy, x0_recips = den, quot
        x0 = sq[0:DH, :, CH:2 * CH]
        h_rows = sq[NEG:P, 0, :]

        maxp = ctx.enter_context(nc.psum_tensor("maxp", [P, 2, CH], F32))
        lin = ctx.enter_context(nc.psum_tensor("lin", [P, 3, 2, CH], F32))
        att_o, att_d = lin[:, 2, 0, :], lin[:, 2, 1, :]

        vec_loaded = sem("vec_loaded")
        weights_loaded = sem("weights_loaded")
        consts_zeroed = sem("consts_zeroed")
        consts_ready = sem("consts_ready")
        bias_sums = sem("bias_sums")
        bias_ready = sem("bias_ready")
        split_step = sem("split_step")
        weights_ready = sem("weights_ready")
        x_next_loaded = sem("x_next_loaded")
        x_loaded = sem("x_loaded")
        squared = [sem(f"squared{k}") for k in range(2)]
        log_ready = [sem(f"log_ready{k}") for k in range(2)]
        guess_ready = [sem(f"guess_ready{k}") for k in range(2)]
        newton = [sem(f"newton{k}") for k in range(2)]
        normed = [sem(f"normed{k}") for k in range(2)]
        normed_hi = [sem(f"normed_hi{k}") for k in range(2)]
        norm_split = [sem(f"norm_split{k}") for k in range(2)]
        job_ready = sem("job_ready")
        ring_ready = sem("ring_ready")
        ring_read = sem("ring_read")
        qk0_hi = sem("qk0_hi")
        qk1_hi = sem("qk1_hi")
        qk1_staged = sem("qk1_staged")
        head_stacked = [[sem(f"head_stacked{grp}_{j}") for j in range(G)] for grp in range(GROUPS)]
        max_ready = sem("max_ready")
        negm_placed = sem("negm_placed")
        ones_ready = sem("ones_ready")
        scores_ready = sem("scores_ready")
        exp_done = sem("exp_done")
        pv_done = sem("pv_done")
        vals_ready = sem("vals_ready")
        h_copied = sem("h_copied")
        vals1_ready = sem("vals1_ready")
        den_copied = sem("den_copied")
        num_copied = sem("num_copied")
        den_log = sem("den_log")
        den_guess = sem("den_guess")
        recip_step = sem("recip_step")
        quot_ready = sem("quot_ready")
        quot_hi = sem("quot_hi")
        heads_ready = sem("heads_ready")
        y_free = sem("y_free")
        hid_ready = sem("hid_ready")
        hid_hi_ready = sem("hid_hi_ready")
        hid_split = sem("hid_split")
        y2_ready = sem("y2_ready")
        y2_hi = sem("y2_hi")
        y2_split = sem("y2_split")
        fg_hi = sem("fg_hi")
        fg_stacked = sem("fg_stacked")
        x0_recip = sem("x0_recip")
        x0_ready = sem("x0_ready")
        x0_hi = sem("x0_hi")
        x0_split = sem("x0_split")
        att_copied = sem("att_copied")

        READ = {}
        for w in range(2):
            READ[f"vals{w}"] = (vals_ready, w + 1, 2)
            READ[f"down{w}"] = (y2_ready, CT * (w + 1), NCH * CT)
        for i in range(8):
            READ[f"up{i // 4}_{i % 4}"] = (hid_ready, 2 * i + 2, 16)
        READ["q1"], READ["k1"] = (qk1_staged, 1, 2), (qk1_staged, 2, 2)
        READ["f"], READ["g"], READ["h"] = (fg_stacked, 1, 2), (fg_stacked, 2, 2), (vals1_ready, 1, 1)

        def wait_read(eng, pl, it, name):
            signal, value, per_image = READ[name]
            eng.wait_ge(signal, (image_next(pl, it) if name in NEXT else it) * per_image + value)

        def wait_pair(eng, pl, it, name):
            before = [j for j in pl.jobs[:pl.jobs.index(name)] if PAIR[j] == PAIR[name]]
            if before:
                wait_read(eng, pl, it, before[-1])

        def wait_stacked(eng, image, grp, head):
            eng.wait_ge(head_stacked[grp][head], (image + 1) * STACK)

        def pair(name):
            return lin[:, PAIR[name], :, :]

        def columns(n):
            return slice(n * CH, n * CH + CH)

        def norm_source(k):
            return xc if k == 0 else y

        def temps(k, n):
            return columns(1 if k == 0 else 1 - n)

        raw_qkv = y[:, :, 0:3 * C]
        raw_w1 = xc[:, :, :]
        prf = pr[:, :, :, :].rearrange("p a b c -> p (a b c)")
        raw_w2 = prf[:, 0:HT * C].rearrange("p (t c) -> p t c", c=C)
        raw_proj = prf[:, 2048:2048 + CT * C].rearrange("p (t c) -> p t c", c=C)
        raw_fgh = prf[:, 2560:2560 + CT * 3 * DH].rearrange("p (t c) -> p t c", c=3 * DH)
        raw_wv = prf[0:3 * DH, 2816:2816 + C]
        scaled_wv = prf[0:3 * DH, 3072:3072 + C]

        block = ctx.enter_context(nc.Block())

        @block.sync
        def _(sp):
            sp.dma_start(vec[:, :], vecs).then_inc(vec_loaded, DMA)
            for t in range(CT):
                rows = slice(t * P, t * P + P)
                sp.dma_start(raw_qkv[:, t, :], wqkv[rows, :]).then_inc(weights_loaded, DMA)
                sp.dma_start(raw_w1[:, t, :], w1[rows, :]).then_inc(weights_loaded, DMA)
                sp.dma_start(raw_proj[:, t, :], wproj[rows, :]).then_inc(weights_loaded, DMA)
                sp.dma_start(raw_fgh[:, t, :], wfgh[rows, :]).then_inc(weights_loaded, DMA)
            sp.dma_start(raw_w2, w2.rearrange("(t p) c -> p t c", p=P)).then_inc(weights_loaded, DMA)
            for r in range(3):
                sp.dma_start(raw_wv[r * DH:r * DH + DH, :], wv).then_inc(weights_loaded, DMA)
            sp.sem_inc(y_free, 1)

            def stack(grp, parts, heads):
                for j in heads:
                    for dst, order in ((qs, (0, 1, 0)), (ks, (2, 2, 3))):
                        for r, part in enumerate(order):
                            sp.dma_start(dst[r * DH:r * DH + DH, G * grp + j, :].bitcast(F32),
                                         parts[part][j * DH:j * DH + DH, :]).then_inc(head_stacked[grp][j], DMA)

            stage1_parts = [stage1[:, i, :].bitcast(F32) for i in range(4)]

            def stack0():
                stack(0, (xc[:, 0, :], xc[:, 1, :], y[:, 0, :], y[:, 1, :]), range(G))

            def stack1(pl, it, heads):
                sp.wait_ge(qk1_staged, image_next(pl, it) * 2 + 2)
                stack(1, stage1_parts, heads)

            def place_negm(pl, it, grp):
                n = ITEMS if grp < 2 else KT
                sp.wait_ge(ring_read, uses_up_to(pl, it, ("turn", grp)))
                row = qs[NEG:NEG + 1, G * grp:G * grp + G, :] if grp < 2 else qs[NEG:NEG + 1, G:G + 1, :]
                sp.dma_start(row.bitcast(F32).rearrange("p a (b c) -> p (a b) c", c=P),
                             negm[0:n, :].bitcast(F32)).then_inc(negm_placed, DMA)

            def image(pl, it):
                if pl.more:
                    following = x[bass.ds(it + 1, 1), :, :].rearrange("a (t p) n -> p (a t) n", p=P)
                    sp.dma_start(xc[:, :, :], following).then_inc(x_next_loaded, DMA)
                if pl.previous:
                    store(pl, it)
                    stack(1, stage1_parts, [0])
                place_negm(pl, it, 1)
                if pl.more:
                    sp.wait_ge(num_copied, it * 4 + 2)
                    stack0()
                    place_negm(pl, it, 0)
                    sp.wait_ge(norm_split[1], it * NCH + NCH)
                    sp.dma_start(xin[:, :, :], following).then_inc(x_loaded, DMA)
                sp.wait_ge(job_ready, job_done(pl, it, "down1"))
                sp.dma_start(ks[NEG:NEG + 1, G:2 * G, :].bitcast(F32), ks[NEG:NEG + 1, 0:G, :].bitcast(F32)
                             ).then_inc(ones_ready, DMA)
                place_negm(pl, it, 2)
                if pl.more:
                    stack1(pl, it, range(1, G))

            def store(pl, it):
                for m in range(CT):
                    sp.wait_ge(ring_read, uses_up_to(pl, it, ("out", m, NCH - 1)))
                    sp.dma_start(out[bass.ds(it - 1, 1), m * P:m * P + P, :].rearrange("a p n -> p (a n)"),
                                 y[:, m, :]).then_inc(y_free, DMA)

            sp.wait_ge(weights_ready, 1)
            for dst, signal in ((xc, x_next_loaded), (xin, x_loaded)):
                sp.dma_start(dst[:, :, :], x[0, :, :].rearrange("(t p) n -> p t n", p=P)).then_inc(signal, DMA)
            sp.wait_ge(ring_read, uses_up_to(FIRST, 0, ("k0", NCH - 1)))
            stack0()
            stack1(FIRST, 0, HEAD_ORDER)
            place_negm(FIRST, 0, 0)
            for j in range(G):
                wait_stacked(sp, 0, 0, j)
            image(START, 0)
            with sp.Fori(1, IMGS - 1) as it:
                image(LOOP, it)
            image(LAST, IMGS - 1)
            store(FINISH, IMGS)
            sp.wait_ge(y_free, 1 + IMGS * CT * DMA)

        @block.gpsimd
        def _(pool):
            nc.gpsimd.memset(avg[:, :], 1.0 / C).then_inc(consts_ready, 1)
            nc.gpsimd.memset(ones[:, :], 1.0).then_inc(consts_ready, 1)
            nc.gpsimd.memset(eps[:, :], EPS).then_inc(consts_ready, 1)
            pool.wait_ge(consts_ready, 3)
            nc.gpsimd.memset(ks[NEG:NEG + 1, :, :].bitcast(F32), 1.0).then_inc(ones_ready, 1)
            pool.wait_ge(ones_ready, 1)
            nc.gpsimd.memset(ident[:, :], 0.0).then_inc(consts_zeroed, 1)
            pool.wait_ge(consts_zeroed, 1)
            nc.gpsimd.affine_select(out=ident[:, :], in_=ident[:, :], compare_op=ALU.not_equal, fill=1.0, base=0,
                                    pattern=[[-1, P]], channel_multiplier=1).then_inc(consts_ready, 1)

        @block.tensor
        def _(pe):
            pe.wait_ge(vec_loaded, DMA)
            pe.wait_ge(weights_loaded, 12 * DMA)
            pe.wait_ge(consts_ready, 4)
            for o in range(3 * CT):
                for t in range(CT):
                    pe.matmul(maxp[:, 0, o:o + 1], raw_qkv[:, t, o * P:o * P + P],
                              vec[:, V_BETA1 + t:V_BETA1 + t + 1], start=t == 0, stop=t == CT - 1)
            for o in range(HT):
                for t in range(CT):
                    pe.matmul(maxp[:, 0, B_FFN + o:B_FFN + o + 1], raw_w1[:, t, o * P:o * P + P],
                              vec[:, V_BETA2 + t:V_BETA2 + t + 1], start=t == 0, stop=t == CT - 1)
            for o in range(CT):
                last = pe.matmul(maxp[:, 0, B_OUT + o:B_OUT + o + 1], raw_wv[0:DH, o * P:o * P + P],
                                 vec[0:DH, V_BH:V_BH + 1], start=True, stop=True)
            last.then_inc(bias_sums, 1)
            pe.wait_ge(bias_ready, 1)
            for o in range(CT):
                for t in range(CT):
                    last = pe.matmul(maxp[:, 1, o:o + 1], raw_proj[:, t, o * P:o * P + P],
                                     bias[:, B_V + t:B_V + t + 1], start=t == 0, stop=t == CT - 1)
            last.then_inc(bias_sums, 1)
            pe.wait_ge(weights_ready, 1)

            def triple(dst, w, cols, src, tok, tiles):
                n_mm = 0
                for t in tiles:
                    for a, b in ((HI, HI), (LO, HI), (HI, LO)):
                        last = pe.matmul(dst, w[:, a, t, cols], src[:, b, t, tok],
                                         start=n_mm == 0, stop=n_mm == 3 * len(tiles) - 1)
                        n_mm += 1
                return last

            def projection(name, w, cols, src, chunks=range(NCH)):
                m = cols.stop - cols.start
                for n in chunks:
                    last = triple(pair(name)[0:m, n, :], w, cols, src, columns(n), range(CT))
                if n == NCH - 1:
                    last.then_inc(job_ready, 1)

            def keys_first(dst, src, k, w):
                n_mm = 0
                for t in range(CT):
                    for a, b in ((HI, HI), (LO, HI), (HI, LO)):
                        last = pe.matmul(dst, src[:, a, t, k * P:k * P + P], w[:, b, t, :],
                                         start=n_mm == 0, stop=n_mm == 3 * CT - 1)
                        n_mm += 1
                return last

            def values(half):
                for i in range(4):
                    last = keys_first(pair(f"vals{half}")[:, i // 2, (i % 2) * C:(i % 2) * C + C], nrm, 4 * half + i,
                                      wqkv_s[:, :, :, 2 * C:3 * C])
                last.then_inc(job_ready, 1)

            def ring(pl, it, segment, part=0, parts=1):
                uses = pl.segments[segment]
                for use in [uses[i] for i in split_evenly(len(uses), parts, part)]:
                    kind, idx = use[0], pl.uses.index(use)
                    bank = maxp[:, idx % 2, :]
                    before = uses_up_to(pl, it, use) - 1
                    if idx == 0 and pl is not FIRST:
                        pe.wait_ge(ring_read, before)
                    elif idx > 0 and (pl is not FIRST or idx > 1):
                        pe.wait_ge(ring_read, before - 1)
                    image = image_next(pl, it)
                    if kind == "max":
                        _, grp, item, n = use
                        j, t = item // KT, item % KT
                        if grp < 2:
                            if item % KT == 0 and n == 0:
                                wait_stacked(pe, image if grp == 0 else it, grp, j)
                            q, k = qs[0:NEG, G * grp + j, :], ks[0:NEG, G * grp + j, :]
                        else:
                            q, k = f_stack[0:NEG], g_stack[0:NEG]
                        last = pe.matmul(bank, q[:, t * P:t * P + P], k[:, columns(n)], start=True, stop=True)
                    elif kind == "turn":
                        n = ITEMS if use[1] < 2 else KT
                        pe.wait_ge(max_ready, place_no(pl, it, use[1]))
                        last = pe.transpose(bank[0:n, 0:P], mxc[:, 0:n], ident[:, :])
                    elif kind == "mean":
                        _, k, n = use
                        if k == 0:
                            pe.wait_ge(x_next_loaded, image * DMA + DMA)
                        else:
                            pe.wait_ge(ring_read, uses_up_to(pl, it, ("proj", n, CT - 1)))
                        for t in range(CT):
                            last = pe.matmul(bank, avg[:, :], norm_source(k)[:, t, columns(n)],
                                             start=t == 0, stop=t == CT - 1)
                    elif kind == "var":
                        _, k, n = use
                        pe.wait_ge(squared[k], (image if k == 0 else it) * NCH + n + 1)
                        for t in range(CT):
                            last = pe.matmul(bank, avg[:, :], sq[:, t, temps(k, n)], start=t == 0, stop=t == CT - 1)
                    elif kind == "out":
                        _, m, n = use
                        pe.wait_ge(x0_split, it)
                        last = pe.matmul(bank, wv_s[:, m * P:m * P + P], x0s[:, columns(n)], start=True, stop=True)
                    elif kind == "proj":
                        _, n, m = use
                        if m == 0:
                            pe.wait_ge(heads_ready, it * 4 + 3 + n)
                        last = triple(bank, wproj_s, slice(m * P, m * P + P), act, columns(n), range(CT))
                    else:
                        first = 0 if kind == "q0" else C
                        pe.wait_ge(norm_split[0], image * NCH + use[1] + 1)
                        last = triple(bank, wqkv_s, slice(first, first + P), nrm, columns(use[1]), range(CT))
                    last.then_inc(ring_ready, 1)

            def half_scores(pl, it, idx, cols):
                if idx >= 2 or pl.previous:
                    pe.wait_ge(exp_done, it * HALVES + idx - 1)
                for i, (k, kt, q, n) in enumerate(cols):
                    last = pe.matmul(lin[:, idx % 2, i, :], k[0:NEG + 1, kt * P:kt * P + P],
                                     q[0:NEG + 1, columns(n)], start=True, stop=True)
                last.then_inc(scores_ready, 1)

            def step_scores(pl, it, g, s, p):
                n, kt = s // KT, s % KT
                heads = [G * g + 2 * p + i for i in range(2)]
                half_scores(pl, it, (g * STEPS + s) * 2 + p, [(ks[:, h, :], kt, qs[:, h, :], n) for h in heads])

            def step_pv(pl, it, g, s, between=lambda i: None):
                n, kt = s // KT, s % KT
                idx = (g * STEPS + s) * 2
                pe.wait_ge(exp_done, it * HALVES + idx + 2)
                if g + s == 0 and pl.previous:
                    pe.wait_ge(att_copied, it)
                elif kt == 0 and g + n > 0:
                    pe.wait_ge(den_copied, it * 4 + 2 * g + n)
                    pe.wait_ge(num_copied, it * 4 + 2 * g + n)
                for j in range(G):
                    if j == G // 2:
                        between(0)
                    pe.matmul(att_o[j * DH:j * DH + DH, :], vals[:, kt, (G * g + j) * DH:(G * g + j + 1) * DH],
                              pr[:, (idx + j // 2) % 4, j % 2, :], start=kt == 0, stop=kt == KT - 1)
                between(1)
                for j in range(G):
                    if j == G // 2:
                        between(2)
                    last = pe.matmul(att_d[j * DH:j * DH + DH, :], ones[:, :],
                                     pr[:, (idx + j // 2) % 4, j % 2, :], start=kt == 0, stop=kt == KT - 1)
                last.then_inc(pv_done, 1)

            def hidden_up(name, n, j):
                for i in range(2):
                    m = 2 * j + i
                    last = triple(pair(name)[:, i, :], w1_s, slice(m * P, m * P + P), act, columns(n), range(CT))
                last.then_inc(job_ready, 1)

            def hidden_down(it, n, beside=lambda: None):
                name = f"down{n}"
                for k in range(HT):
                    if k == 2:
                        beside()
                    if k % 2 == 0:
                        pe.wait_ge(hid_split, it * 2 * 4 + n * 4 + k // 2 + 1)
                    for m in range(CT):
                        for i, (a, b) in enumerate(((HI, hid_hi), (LO, hid_hi), (HI, hid_lo))):
                            last = pe.matmul(pair(name)[:, m, :], w2_s[:, a, k, m * P:m * P + P], b[:, k, :],
                                             start=k == 0 and i == 0, stop=k == HT - 1 and i == 2)
                last.then_inc(job_ready, 1)

            def image(pl, it):
                pe.wait_ge(negm_placed, (pl.places_before + it * len(LOOP.places)) * DMA)
                pe.wait_ge(vals_ready, it * 2 + 2)
                for g in range(GROUPS):
                    if g == 1:
                        pe.wait_ge(negm_placed, place_no(pl, it, 1) * DMA)
                    for s in range(STEPS):
                        def beside(part):
                            if (g, s) == (0, STEPS - 1):
                                part = part * 6
                            if part < 6:
                                ring(pl, it, g * STEPS + s, part, 1 if (g, s) == (0, STEPS - 1) else 6)

                        for p in range(2):
                            step_scores(pl, it, g, s, p)
                            beside(p)
                        if s > 0:
                            step_pv(pl, it, g, s - 1, lambda i: beside(2 + i))
                        else:
                            for i in range(3):
                                beside(2 + i)
                        beside(5)
                    step_pv(pl, it, g, STEPS - 1)

                def up(n, j):
                    wait_pair(pe, pl, it, f"up{n}_{j}")
                    hidden_up(f"up{n}_{j}", n, j)

                pe.wait_ge(exp_done, it * HALVES + L0_HALVES)
                if pl.more:
                    values(0)
                    ring(pl, it, "turn", 0, 2)
                    values(1)
                    ring(pl, it, "turn", 1, 2)
                pe.wait_ge(den_copied, it * 4 + 4)
                pe.wait_ge(num_copied, it * 4 + 4)
                pe.wait_ge(norm_split[1], it * NCH + 1)
                up(0, 0)
                up(0, 1)
                up(0, 2)
                ring(pl, it, "proj")
                up(0, 3)
                ring(pl, it, "mean2")
                wait_pair(pe, pl, it, "down0")
                hidden_down(it, 0, lambda: ring(pl, it, "var2"))
                pe.wait_ge(norm_split[1], it * NCH + NCH)
                for j in range(4):
                    up(1, j)
                wait_pair(pe, pl, it, "down1")
                hidden_down(it, 1)

                wait_pair(pe, pl, it, "f")
                wait_pair(pe, pl, it, "g")
                for n in range(NCH):
                    pe.wait_ge(y2_split, it * NCH + n + 1)
                    projection("f", wfhg_s, slice(0, 4 * DH), act, [n])
                    projection("g", wfhg_s, slice(4 * DH, 7 * DH), act, [n])
                pe.wait_ge(fg_stacked, it * 2 + 2)
                ring(pl, it, "layer1", 0, 5)
                pe.wait_ge(h_copied, it + 1)
                if pl.more:
                    wait_pair(pe, pl, it, "q1")
                for n in range(NCH):
                    if pl.more:
                        projection("q1", wqkv_s, slice(P, C), nrm, [n])
                    ring(pl, it, "layer1", 1 + n, 5)
                wait_pair(pe, pl, it, "h")
                for k in range(KT):
                    last = pe.matmul(pair("h")[:, 0, k * DH:k * DH + DH], h_rows[:, k * P:k * P + P],
                                     ident[NEG:P, NEG:P], start=True, stop=True)
                last.then_inc(job_ready, 1)
                ring(pl, it, "layer1", 3, 5)
                if pl.more:
                    wait_pair(pe, pl, it, "k1")
                    projection("k1", wqkv_s, slice(C + P, 2 * C), nrm, [0])
                ring(pl, it, "layer1", 4, 5)
                ring(pl, it, "turn1")
                if pl.more:
                    projection("k1", wqkv_s, slice(C + P, 2 * C), nrm, [1])
                    wait_read(pe, pl, it, "k1")
                wait_read(pe, pl, it, "h")
                pe.wait_ge(ones_ready, 1 + (it + 1) * DMA)
                pe.wait_ge(negm_placed, place_no(pl, it, 2) * DMA)
                for kt in range(KT + 1):
                    if kt < KT:
                        half_scores(pl, it, L0_HALVES + kt, [(g_stack, kt, f_stack, n) for n in range(NCH)])
                    if kt > 0:
                        k = kt - 1
                        idx = L0_HALVES + k
                        pe.wait_ge(exp_done, it * HALVES + idx + 1)
                        for n in range(NCH):
                            pe.matmul(att_o[n * DH:n * DH + DH, :], vals1[:, k, :], pr[:, idx % 4, n, :],
                                      start=k == 0, stop=k == KT - 1)
                        for n in range(NCH):
                            last = pe.matmul(att_o[2 * DH + n * DH:3 * DH + n * DH, :], ones[:, :], pr[:, idx % 4, n, :],
                                             start=k == 0, stop=k == KT - 1)
                        last.then_inc(pv_done, 1)

            pe.wait_ge(ones_ready, 1)
            for segment in ("mean", "mean, var", "var", "qk"):
                ring(FIRST, 0, segment)
            values(0)
            values(1)
            wait_pair(pe, FIRST, 0, "q1")
            projection("q1", wqkv_s, slice(P, C), nrm)
            wait_pair(pe, FIRST, 0, "k1")
            projection("k1", wqkv_s, slice(C + P, 2 * C), nrm)
            ring(FIRST, 0, "maxima")
            wait_read(pe, FIRST, 0, "k1")
            image(START, 0)
            with pe.Fori(1, IMGS - 1) as it:
                image(LOOP, it)
            image(LAST, IMGS - 1)
            ring(FINISH, IMGS, "out")

        @block.scalar
        def _(sc):
            sc.preload_act_table_set("natural_log_exp_and_others")
            sc.wait_ge(weights_ready, 1)
            sc.wait_ge(consts_ready, 4)

            def norm_square(pl, it, k, n):
                image = image_next(pl, it) if k == 0 else it
                sc.wait_ge(ring_read, uses_up_to(pl, it, ("mean", k, n)))
                nc.scalar.activation(sq[:, :, temps(k, n)], xc[:, :, columns(n)], ACT.Square).then_inc(squared[k], 1)

            def norm_guess(pl, it, k, n):
                image = image_next(pl, it) if k == 0 else it
                var, guess = sq[:, 0, temps(k, n)], sq[:, 1, temps(k, n)]
                sc.wait_ge(ring_read, uses_up_to(pl, it, ("var", k, n)))
                nc.scalar.activation(guess, var, ACT.Ln).then_inc(log_ready[k], 1)
                sc.wait_ge(log_ready[k], image * NCH + n + 1)
                nc.scalar.activation(guess, guess, ACT.Exp, scale=-0.5).then_inc(guess_ready[k], 1)

            def norm_hi(pl, it, k, n):
                image = image_next(pl, it) if k == 0 else it
                dst = nrm if k == 0 else act
                sc.wait_ge(normed[k], image * NCH + n + 1)
                nc.scalar.copy(dst[:, HI, :, columns(n)], xc[:, :, columns(n)]).then_inc(normed_hi[k], 1)

            def qk0_evac(pl, it, name, n):
                dst, col = (q0_stage, B_QK) if name == "q0" else (k0_stage, B_QK + 2)
                use = (name, n)
                if use == QK0[1] and pl is not FIRST:
                    sc.wait_ge(recip_step, it * 8 + 2)
                sc.wait_ge(ring_ready, uses_up_to(pl, it, use))
                nc.scalar.activation(dst[:, 0, columns(n)], maxp[:, pl.uses.index(use) % 2, :], ACT.Identity,
                                     bias=bias[:, col:col + 1]).then_inc(qk0_hi, 1)

            def qk1_evac(pl, it, name):
                slot, col = (0, B_QK + 1) if name == "q1" else (2, B_QK + 3)
                sc.wait_ge(job_ready, job_done(pl, it, name))
                nc.scalar.activation(stage1[:, slot, :], pair(name), ACT.Identity,
                                     bias=bias[:, col:col + 1]).then_inc(qk1_hi, 1)

            def vals_evac(pl, it, half):
                sc.wait_ge(job_ready, job_done(pl, it, f"vals{half}"))
                nc.scalar.copy(vals[:, 4 * half:4 * half + 4, :], pair(f"vals{half}")).then_inc(vals_ready, 1)

            def copy_att(it):
                sc.wait_ge(pv_done, it * PV)
                nc.scalar.copy(att_copy, att_o).then_inc(att_copied, 1)

            def x0_split_hi(it):
                sc.wait_ge(x0_ready, it * NCH)
                for r in (0, 2):
                    nc.scalar.copy(x0s[r * DH:r * DH + DH, :].rearrange("p (a b) -> p a b", b=CH), x0).then_inc(x0_hi, 1)

            def half_exp(pl, it, idx, scale):
                sc.wait_ge(scores_ready, it * HALVES + idx + 1)
                if idx < 4:
                    if pl.previous:
                        sc.wait_ge(pv_done, it * PV - 3 + idx)
                elif idx < L0_HALVES:
                    sc.wait_ge(pv_done, it * PV + (idx - 4) // 2 + 1)
                elif idx >= L0_HALVES + 4:
                    sc.wait_ge(pv_done, it * PV + GROUPS * STEPS + idx - 4 - L0_HALVES + 1)
                nc.scalar.activation(pr[:, idx % 4, :, :], lin[:, idx % 2, :, :], ACT.Exp,
                                     scale=scale).then_inc(exp_done, 1)

            def den_copy(it, g, n):
                sc.wait_ge(pv_done, it * PV + (g * NCH + n + 1) * KT)
                if g + n > 0:
                    sc.wait_ge(quot_ready, it * 4 + 2 * g + n)
                nc.scalar.copy(den, att_d).then_inc(den_copied, 1)

            def den_recip(it, g, n):
                k = it * 4 + 2 * g + n
                sc.wait_ge(den_copied, k + 1)
                if g + n == 0:
                    sc.wait_ge(y_free, it * CT * DMA + 1)
                nc.scalar.activation(guess(g, n), den, ACT.Ln).then_inc(den_log, 1)
                sc.wait_ge(den_log, k + 1)
                nc.scalar.activation(guess(g, n), guess(g, n), ACT.Exp, scale=-1.0).then_inc(den_guess, 1)

            def quot_split(it, g, n):
                if g + n == 0:
                    for j in range(G):
                        wait_stacked(sc, it, 1, j)
                sc.wait_ge(quot_ready, it * 4 + 2 * g + n + 1)
                nc.scalar.copy(act[:, HI, g, columns(n)], quot).then_inc(quot_hi, 1)

            def y2_split_hi(it, n):
                sc.wait_ge(y2_ready, it * 2 * CT + CT * (n + 1))
                nc.scalar.copy(act[:, HI, :, columns(n)], y[:, :, columns(n)]).then_inc(y2_hi, 1)

            def beside(pl, it, s, at):
                when = (s, at)
                if pl.previous:
                    if when == (0, 1):
                        copy_att(it)
                    elif when == (2, 1):
                        x0_split_hi(it)
                if pl.more:
                    if when == (3, 2):
                        if pl.previous:
                            sc.wait_ge(x0_split, it)
                        norm_square(pl, it, 0, 0)
                    elif when == (4, 2):
                        norm_guess(pl, it, 0, 0)
                    elif when == (7, 2):
                        norm_hi(pl, it, 0, 0)
                    elif when == (8, 1):
                        norm_square(pl, it, 0, 1)
                    elif when == (9, 2):
                        norm_guess(pl, it, 0, 1)
                    elif when == (12, 2):
                        norm_hi(pl, it, 0, 1)
                    elif at == 0 and s in (10, 13, 14, 15):
                        qk0_evac(pl, it, *QK0[(10, 13, 14, 15).index(s)])
                for (g, n), copy_at, guess_at, split_at in (((0, 0), KT, (KT + 1, 1), (KT + 5, 1)),
                                                            ((0, 1), STEPS, (STEPS + 1, 1), (STEPS + 4, 1)),
                                                            ((1, 0), STEPS + KT, (STEPS + KT, 2), (STEPS + KT + 2, 1))):
                    if when == (copy_at, 2):
                        den_copy(it, g, n)
                    if when == guess_at:
                        den_recip(it, g, n)
                    elif when == split_at:
                        quot_split(it, g, n)
                if when == (STEPS + 13, 2):
                    norm_square(pl, it, 1, 0)
                elif when == (STEPS + 14, 2):
                    norm_guess(pl, it, 1, 0)

            def hidden(pl, it, i):
                n, j = i // 4, i % 4
                hid32 = pr[:, j, :, :]
                sc.wait_ge(job_ready, job_done(pl, it, f"up{n}_{j}"))
                if i >= 4:
                    sc.wait_ge(hid_split, it * 8 + i - 3)
                for e in range(2):
                    nc.scalar.activation(hid32[:, e, :], pair(f"up{n}_{j}")[:, e, :],
                                         ACT.Relu, bias=bias[:, B_FFN + 2 * j + e:B_FFN + 2 * j + e + 1]
                                         ).then_inc(hid_ready, 1)
                sc.wait_ge(hid_ready, it * 16 + 2 * i + 2)
                if i == 4:
                    sc.wait_ge(job_ready, job_done(pl, it, "down0"))
                nc.scalar.copy(hid_hi[:, 2 * j:2 * j + 2, :], hid32).then_inc(hid_hi_ready, 1)

            def image(pl, it):
                for s in range(GROUPS * STEPS):
                    beside(pl, it, s, 0)
                    half_exp(pl, it, 2 * s, SCALE)
                    beside(pl, it, s, 1)
                    half_exp(pl, it, 2 * s + 1, SCALE)
                    beside(pl, it, s, 2)
                den_copy(it, 1, 1)
                norm_hi(pl, it, 1, 0)
                den_recip(it, 1, 1)
                if pl.more:
                    vals_evac(pl, it, 0)
                    vals_evac(pl, it, 1)
                hidden(pl, it, 0)
                quot_split(it, 1, 1)
                hidden(pl, it, 1)
                hidden(pl, it, 2)
                hidden(pl, it, 3)
                norm_square(pl, it, 1, 1)
                norm_guess(pl, it, 1, 1)
                norm_hi(pl, it, 1, 1)
                for i in range(4, 8):
                    hidden(pl, it, i)
                y2_split_hi(it, 0)
                y2_split_hi(it, 1)
                for i, (name, dst) in enumerate((("f", f_stack), ("g", g_stack))):
                    sc.wait_ge(job_ready, job_done(pl, it, name))
                    nc.scalar.activation(dst[0:3 * DH], pair(name)[0:3 * DH], ACT.Identity,
                                         bias=vec[0:3 * DH, V_BF + i:V_BF + i + 1]).then_inc(fg_hi, 1)
                nc.scalar.copy(h_rows.rearrange("p (a b) -> p a b", b=CH), pair("f")[NEG:P]).then_inc(h_copied, 1)
                if pl.more:
                    qk1_evac(pl, it, "q1")
                sc.wait_ge(job_ready, job_done(pl, it, "h"))
                nc.scalar.copy(vals1[:, :, :], pair("h")[:, 0, 0:KT * DH].rearrange("p (a c) -> p a c", c=DH)
                               ).then_inc(vals1_ready, 1)
                if pl.more:
                    qk1_evac(pl, it, "k1")
                for kt in range(KT):
                    half_exp(pl, it, L0_HALVES + kt, 1.0)

            for n in range(NCH):
                norm_square(FIRST, 0, 0, n)
                norm_guess(FIRST, 0, 0, n)
                norm_hi(FIRST, 0, 0, n)
            for use in QK0:
                qk0_evac(FIRST, 0, *use)
            vals_evac(FIRST, 0, 0)
            vals_evac(FIRST, 0, 1)
            qk1_evac(FIRST, 0, "q1")
            qk1_evac(FIRST, 0, "k1")
            image(START, 0)
            with sc.Fori(1, IMGS - 1) as it:
                image(LOOP, it)
            image(LAST, IMGS - 1)
            copy_att(IMGS)
            x0_split_hi(IMGS)

        @block.vector
        def _(ve):
            V = nc.vector
            ve.wait_ge(vec_loaded, DMA)
            ve.wait_ge(weights_loaded, 12 * DMA)
            ve.wait_ge(bias_sums, 1)
            V.tensor_copy(bias[:, B_QK:B_V + CT], maxp[:, 0, B_QK:B_V + CT]).then_inc(bias_ready, 1)
            V.tensor_tensor(bias[:, B_FFN:B_FFN + HT], maxp[:, 0, B_FFN:B_FFN + HT], vec[:, V_B1:V_B1 + HT], ALU.add)
            V.tensor_tensor(bias[:, B_OUT:B_OUT + CT], maxp[:, 0, B_OUT:B_OUT + CT], vec[:, V_BV:V_BV + CT],
                            ALU.add).then_inc(split_step, 1)
            ve.wait_ge(split_step, 1)
            V.tensor_scalar(bias[:, B_OUT:B_OUT + CT], bias[:, B_OUT:B_OUT + CT], vec[:, V_GAMMA:V_GAMMA + 1], None,
                            ALU.mult)
            ve.wait_ge(bias_sums, 2)
            V.tensor_tensor(bias[:, B_PROJ:B_PROJ + CT], maxp[:, 1, 0:CT], vec[:, V_BPROJ:V_BPROJ + CT], ALU.add)
            steps = 1
            for raw, dst, gain in ((raw_qkv, wqkv_s, V_G1), (raw_w1, w1_s, V_G2)):
                for t in range(CT):
                    V.tensor_scalar(raw[:, t, :], raw[:, t, :], vec[:, gain + t:gain + t + 1], None,
                                    ALU.mult).then_inc(split_step, 1)
                steps += CT
            V.tensor_scalar(scaled_wv, raw_wv, vec[0:3 * DH, V_GAMMA:V_GAMMA + 1], None, ALU.mult).then_inc(split_step, 1)
            steps += 1
            ve.wait_ge(split_step, steps)
            splits = [(raw_qkv, wqkv_s[:, :, :, :]), (raw_w1, w1_s[:, :, :, :]), (raw_w2, w2_s[:, :, :, :]),
                      (raw_proj, wproj_s[:, :, :, :])]
            splits += [(raw_fgh[:, :, i * DH:i * DH + DH], wfhg_s[:, :, :, to * DH:to * DH + DH])
                       for to, i in enumerate((0, 0, 0, 2, 1, 1, 1))]
            for raw, dst in splits:
                V.tensor_copy(dst[:, HI], raw).then_inc(split_step, 1)
            V.tensor_copy(wv_s[:, :], scaled_wv).then_inc(split_step, 1)
            steps += len(splits) + 1
            ve.wait_ge(split_step, steps)
            for raw, dst in splits:
                V.tensor_tensor(dst[:, LO], raw, dst[:, HI].bitcast(F32), ALU.subtract)
            V.tensor_tensor(wv_s[2 * DH:3 * DH, :], scaled_wv[2 * DH:3 * DH, :], wv_s[2 * DH:3 * DH, :].bitcast(F32),
                            ALU.subtract).then_inc(weights_ready, 1)

            def ring(pl, it, segment, part=0, parts=1, beside=()):
                uses = [pl.segments[segment][i] for i in split_evenly(len(pl.segments[segment]), parts, part)]
                if not uses:
                    for work in beside:
                        other(pl, it, *work)
                for place, use in enumerate(uses):
                    take(pl, it, use)
                    for i in split_evenly(len(beside), len(uses), place):
                        other(pl, it, *beside[i])

            def other(pl, it, kind, a, b, i=0):
                if kind == "scale":
                    norm_scale(pl, it, a, b, i)
                elif kind == "lo":
                    norm_lo(pl, it, a, b)
                elif kind == "numerators":
                    num_copy(it, a, b)
                elif kind == "quotient":
                    quotient(it, a, b, i)
                elif kind == "heads":
                    quotient_lo(it, a, b)
                elif kind == "x0 reciprocal":
                    x0_reciprocal(it, a)
                elif kind == "x0":
                    x0_quotient(it, a)
                elif kind == "x0 lo":
                    x0_lo(it)

            def x0_reciprocal(it, part):
                ve.wait_ge(att_copied, it)
                cols = slice(part * CH // NCH, (part + 1) * CH // NCH)
                V.reciprocal(x0_recips[0:NCH * DH, cols], att_copy[NCH * DH:2 * NCH * DH, cols]).then_inc(x0_recip, 1)

            def x0_quotient(it, n):
                ve.wait_ge(x0_recip, it * NCH)
                rows = slice(n * DH, n * DH + DH)
                V.tensor_tensor(x0[:, n, :], att_copy[rows], x0_recips[rows], ALU.mult).then_inc(x0_ready, 1)

            def x0_lo(it):
                ve.wait_ge(x0_hi, it * 2)
                V.tensor_tensor(x0s[DH:2 * DH, :].rearrange("p (a b) -> p a b", b=CH), x0,
                                x0s[0:DH, :].rearrange("p (a b) -> p a b", b=CH).bitcast(F32),
                                ALU.subtract).then_inc(x0_split, 1)

            def take(pl, it, use):
                if True:
                    kind, idx = use[0], pl.uses.index(use)
                    bank = maxp[:, idx % 2, :]
                    no = uses_up_to(pl, it, use)
                    if kind == "max":
                        _, grp, item, n = use
                        ve.wait_ge(ring_ready, no)
                        V.tensor_reduce(mx[:, n, item:item + 1], bank, AX.X, ALU.max).then_inc(ring_read, 1)
                        if use == [u for u in pl.uses if u[:2] == ("max", grp)][-1]:
                            m = ITEMS if grp < 2 else KT
                            ve.wait_ge(ring_read, no)
                            V.tensor_tensor(mxc[:, 0:m], mx[:, 0, 0:m], mx[:, 1, 0:m],
                                            ALU.max).then_inc(max_ready, 1)
                    elif kind == "turn":
                        n = ITEMS if use[1] < 2 else KT
                        ve.wait_ge(ring_ready, no)
                        if pl is not FIRST:
                            ve.wait_ge(negm_placed, (place_no(pl, it, use[1]) - 1) * DMA)
                        V.tensor_scalar(negm[0:n, :], bank[0:n, 0:P], -1.0, None, ALU.mult).then_inc(ring_read, 1)
                    elif kind == "mean":
                        n = use[2]
                        ve.wait_ge(ring_ready, no)
                        for t in range(CT):
                            last = V.tensor_tensor(xc[:, t, columns(n)], norm_source(use[1])[:, t, columns(n)], bank,
                                                   ALU.subtract)
                        last.then_inc(ring_read, 1)
                    elif kind == "var":
                        ve.wait_ge(ring_ready, no)
                        V.tensor_scalar(sq[:, 0, temps(*use[1:])], bank, EPS, None, ALU.add).then_inc(ring_read, 1)
                    elif kind == "out":
                        _, m, n = use
                        ve.wait_ge(ring_ready, no)
                        V.scalar_tensor_tensor(out=y[:, m, columns(n)], in0=bank, scalar=bias[:, B_OUT + m:B_OUT + m + 1],
                                               in1=y[:, m, columns(n)], op0=ALU.add, op1=ALU.add).then_inc(ring_read, 1)
                    elif kind == "proj":
                        _, n, m = use
                        if n == 0 and m == 0:
                            if pl.more:
                                for j in range(G):
                                    wait_stacked(ve, it + 1, 0, j)
                            ve.wait_ge(y_free, it * CT * DMA + 1)
                            ve.wait_ge(x_loaded, it * DMA + DMA)
                        ve.wait_ge(ring_ready, no)
                        V.scalar_tensor_tensor(out=y[:, m, columns(n)], in0=bank,
                                               scalar=bias[:, B_PROJ + m:B_PROJ + m + 1], in1=xin[:, m, columns(n)],
                                               op0=ALU.add, op1=ALU.add).then_inc(ring_read, 1)
                    else:
                        n = use[1]
                        dst, col = (q0_stage, B_QK) if kind == "q0" else (k0_stage, B_QK + 2)
                        ve.wait_ge(qk0_hi, image_next(pl, it) * len(QK0) + QK0.index(use) + 1)
                        V.scalar_tensor_tensor(out=dst[:, 1, columns(n)], in0=bank, scalar=bias[:, col:col + 1],
                                               in1=dst[:, 0, columns(n)].bitcast(F32),
                                               op0=ALU.add, op1=ALU.subtract).then_inc(ring_read, 1)

            def norm_scale(pl, it, k, n, part):
                image = image_next(pl, it) if k == 0 else it
                a, r = sq[:, 0, temps(k, n)], sq[:, 1, temps(k, n)]
                done = (image * NCH + n) * 3 + part
                if part == 0:
                    ve.wait_ge(guess_ready[k], image * NCH + n + 1)
                    V.scalar_tensor_tensor(out=a, in0=a, scalar=-0.5, in1=r, op0=ALU.mult,
                                           op1=ALU.mult).then_inc(newton[k], 1)
                elif part == 1:
                    ve.wait_ge(newton[k], done)
                    V.tensor_tensor(a, a, r, ALU.mult).then_inc(newton[k], 1)
                elif part == 2:
                    ve.wait_ge(newton[k], done)
                    V.scalar_tensor_tensor(out=a, in0=a, scalar=1.5, in1=r, op0=ALU.add,
                                           op1=ALU.mult).then_inc(newton[k], 1)
                else:
                    t = part - 3
                    ve.wait_ge(newton[k], (image * NCH + n) * 3 + 3)
                    last = V.tensor_tensor(xc[:, t, columns(n)], xc[:, t, columns(n)], a, ALU.mult)
                    if t == CT - 1:
                        last.then_inc(normed[k], 1)

            def norm_lo(pl, it, k, n):
                image = image_next(pl, it) if k == 0 else it
                dst = nrm if k == 0 else act
                ve.wait_ge(normed_hi[k], image * NCH + n + 1)
                V.tensor_tensor(dst[:, LO, :, columns(n)], xc[:, :, columns(n)], dst[:, HI, :, columns(n)].bitcast(F32),
                                ALU.subtract).then_inc(norm_split[k], 1)

            def qk1_lo(pl, it, name):
                i, slot, col = (0, 0, B_QK + 1) if name == "q1" else (1, 2, B_QK + 3)
                ve.wait_ge(qk1_hi, image_next(pl, it) * 2 + i + 1)
                V.scalar_tensor_tensor(out=stage1[:, slot + 1, :], in0=pair(name).rearrange("p a b -> p (a b)"),
                                       scalar=bias[:, col:col + 1], in1=stage1[:, slot, :].bitcast(F32),
                                       op0=ALU.add, op1=ALU.subtract).then_inc(qk1_staged, 1)

            def num_copy(it, g, n):
                ve.wait_ge(pv_done, it * PV + (g * NCH + n + 1) * KT)
                if g + n > 0:
                    ve.wait_ge(heads_ready, it * 4 + 2 * g + n)
                V.tensor_copy(quot, att_o).then_inc(num_copied, 1)

            def quotient(it, g, n, part):
                k = it * 4 + 2 * g + n
                if part == 0:
                    ve.wait_ge(den_guess, k + 1)
                    V.tensor_tensor(den, den, guess(g, n), ALU.mult).then_inc(recip_step, 1)
                elif part == 1:
                    ve.wait_ge(recip_step, 2 * k + 1)
                    V.scalar_tensor_tensor(out=den, in0=den, scalar=-2.0, in1=guess(g, n), op0=ALU.add,
                                           op1=ALU.mult).then_inc(recip_step, 1)
                else:
                    ve.wait_ge(recip_step, 2 * k + 2)
                    V.scalar_tensor_tensor(out=quot, in0=quot, scalar=-1.0, in1=den, op0=ALU.mult,
                                           op1=ALU.mult).then_inc(quot_ready, 1)

            def quotient_lo(it, g, n):
                ve.wait_ge(quot_hi, it * 4 + 2 * g + n + 1)
                V.tensor_tensor(act[:, LO, g, columns(n)], quot, act[:, HI, g, columns(n)].bitcast(F32),
                                ALU.subtract).then_inc(heads_ready, 1)

            def hidden_lo(it, i):
                j = i % 4
                ve.wait_ge(hid_hi_ready, it * 8 + i + 1)
                V.tensor_tensor(hid_lo[:, 2 * j:2 * j + 2, :], pr[:, j, :, :],
                                hid_hi[:, 2 * j:2 * j + 2, :].bitcast(F32), ALU.subtract).then_inc(hid_split, 1)

            def feed_forward_sum(pl, it, n):
                ve.wait_ge(job_ready, job_done(pl, it, f"down{n}"))
                for m in range(CT):
                    V.scalar_tensor_tensor(out=y[:, m, columns(n)], in0=pair(f"down{n}")[:, m, :],
                                           scalar=vec[:, V_B2 + m:V_B2 + m + 1], in1=y[:, m, columns(n)],
                                           op0=ALU.add, op1=ALU.add).then_inc(y2_ready, 1)

            def image(pl, it):
                for s in range(GROUPS * STEPS):
                    ring(pl, it, s, beside=(PREVIOUS.get(s, []) if pl.previous else [])
                         + (NEXT_NORM.get(s, []) if pl.more else []) + QUOTIENTS.get(s, []))

                for part in (3, 4):
                    norm_scale(pl, it, 1, 0, part)
                num_copy(it, 1, 1)
                ring(pl, it, "turn", 0, 2)
                norm_lo(pl, it, 1, 0)
                ring(pl, it, "turn", 1, 2)
                for part in range(3):
                    quotient(it, 1, 1, part)
                hidden_lo(it, 0)
                quotient_lo(it, 1, 1)
                hidden_lo(it, 1)
                hidden_lo(it, 2)
                ring(pl, it, "proj")
                hidden_lo(it, 3)
                ring(pl, it, "mean2")
                ring(pl, it, "var2")
                for part in range(5):
                    norm_scale(pl, it, 1, 1, part)
                norm_lo(pl, it, 1, 1)
                feed_forward_sum(pl, it, 0)
                for i in range(4, 8):
                    hidden_lo(it, i)
                y2_split_lo(it, 0)
                feed_forward_sum(pl, it, 1)
                y2_split_lo(it, 1)

                for i, (name, dst, row, col) in enumerate((("f", f_stack, 1, V_BF), ("g", g_stack, 2, V_BG))):
                    ve.wait_ge(fg_hi, it * 2 + i + 1)
                    rows = slice(row * DH, row * DH + DH)
                    V.scalar_tensor_tensor(out=dst[rows], in0=pair(name)[rows].rearrange("p a b -> p (a b)"),
                                           scalar=vec[rows, col:col + 1], in1=dst[rows].bitcast(F32),
                                           op0=ALU.add, op1=ALU.subtract).then_inc(fg_stacked, 1)
                ring(pl, it, "layer1")
                if pl.more:
                    qk1_lo(pl, it, "q1")
                ring(pl, it, "turn1")
                if pl.more:
                    qk1_lo(pl, it, "k1")

            def y2_split_lo(it, n):
                ve.wait_ge(y2_hi, it * NCH + n + 1)
                V.tensor_tensor(act[:, LO, :, columns(n)], y[:, :, columns(n)], act[:, HI, :, columns(n)].bitcast(F32),
                                ALU.subtract).then_inc(y2_split, 1)

            ve.wait_ge(weights_ready, 1)
            ring(FIRST, 0, "mean")
            ring(FIRST, 0, "mean, var")
            for part in range(5):
                norm_scale(FIRST, 0, 0, 0, part)
            norm_lo(FIRST, 0, 0, 0)
            ring(FIRST, 0, "var")
            for part in range(5):
                norm_scale(FIRST, 0, 0, 1, part)
            norm_lo(FIRST, 0, 0, 1)
            ring(FIRST, 0, "qk")
            qk1_lo(FIRST, 0, "q1")
            qk1_lo(FIRST, 0, "k1")
            ring(FIRST, 0, "maxima")
            image(START, 0)
            with ve.Fori(1, IMGS - 1) as it:
                image(LOOP, it)
            image(LAST, IMGS - 1)
            for works in PREVIOUS.values():
                for work in works:
                    other(FINISH, IMGS, *work)
            ring(FINISH, IMGS, "out")


def kernel(**inputs):
    import concourse.bacc as bacc
    import numpy as np
    from concourse.bass_utils import run_bass_kernel_spmd

    a = {k: np.asarray(v) for k, v in inputs.items()}
    x = np.ascontiguousarray(a["x"])
    imgs, c, hh, ww = x.shape

    def columns(v):
        v = np.tile(v, P // v.size) if v.size < P else v
        return v.reshape(-1, P).T

    vecs = np.concatenate([columns(a[n]) for n in (
        "L0_conv_g1", "L0_conv_beta1", "L0_conv_g2", "L0_conv_beta2", "L0_conv_b_proj", "L0_conv_b1", "L0_conv_b2",
        "L1_conv_bv", "L1_conv_bf", "L1_conv_bg", "L1_conv_bh", "L1_conv_gamma")], axis=1)
    arrays = {
        "x": x.reshape(imgs, c, hh * ww),
        "wqkv": a["L0_conv_w_qkv"].T,
        "wproj": a["L0_conv_w_proj"].T,
        "w1": a["L0_conv_w1"].T,
        "w2": a["L0_conv_w2"].T,
        "wfgh": np.concatenate([a["L1_conv_wf"], a["L1_conv_wg"], a["L1_conv_wh"]], axis=0).T,
        "wv": a["L1_conv_wv"].T,
        "vecs": vecs,
    }
    arrays = {f"in_{k}": np.ascontiguousarray(v) for k, v in arrays.items()}
    nc = bacc.Bacc("TRN2", target_bir_lowering=False, num_devices=1)
    args = [nc.dram_tensor(k, v.shape, F32, kind="ExternalInput").ap() for k, v in arrays.items()]
    args.append(nc.dram_tensor("out_y", (imgs, c, hh * ww), F32, kind="ExternalOutput").ap())
    attention_layers(nc, *args)
    r = run_bass_kernel_spmd(nc, [arrays], core_ids=[0])
    return r.results[0]["out_y"].reshape(x.shape)
```

```python
from contextlib import ExitStack

import concourse.bass as bass
from concourse import mybir

F32 = mybir.dt.float32
F32R = mybir.dt.float32r
ALU = mybir.AluOpType
ACT = mybir.ActivationFunctionType
AX = mybir.AxisListType

P = 128
DH = 32
HI, LO = 0, 1
NEG = 3 * DH
CH = 512
EPS = 1e-5
DMA = 16

V_G1, V_BETA1, V_G2, V_BETA2, V_BPROJ, V_B1, V_B2, V_BV, V_BF, V_BG, V_BH, V_GAMMA, V_COLS = (
    0, 2, 4, 6, 8, 10, 18, 20, 22, 23, 24, 25, 26)
B_QK, B_V, B_PROJ, B_FFN, B_OUT, B_COLS = 0, 4, 6, 8, 16, 18


def split_evenly(n, parts, i):
    return range(n * i // parts, n * (i + 1) // parts)


class Plan:

    def __init__(self, jobs, segments, places, more=True, previous=True, jobs_before=0, uses_before=0, places_before=0):
        self.jobs, self.segments, self.places = jobs, segments, places
        self.uses = [use for part in segments.values() for use in part]
        self.more, self.previous = more, previous
        self.jobs_before, self.uses_before, self.places_before = jobs_before, uses_before, places_before


def attention_layers(nc, x, wqkv, wproj, w1, w2, wfgh, wv, vecs, out):
    IMGS, C, N = x.shape
    CT = C // P
    KT = N // P
    NCH = N // CH
    HEADS = C // DH
    G = P // DH
    GROUPS = HEADS // G
    HID = w1.shape[1]
    HT = HID // P
    SCALE = float(DH) ** -0.5
    assert (CT, KT, NCH, G, GROUPS, HT) == (2, 8, 2, 4, 2, 8)

    STEPS = NCH * KT
    L0_HALVES = GROUPS * STEPS * 2
    HALVES = L0_HALVES + KT
    PV = GROUPS * STEPS + KT
    ITEMS = G * KT
    STACK = 6 * DMA

    NEXT = ("vals0", "vals1", "q1", "k1")
    LOOP_JOBS = (["vals0", "vals1"] + [f"up0_{j}" for j in range(4)] + ["down0"]
                 + [f"up1_{j}" for j in range(4)] + ["down1", "f", "g", "q1", "h", "k1"])
    PAIR = {name: i % 3 for i, name in enumerate(LOOP_JOBS)}
    NJ = len(LOOP_JOBS)

    def maxima(grp, items):
        return [("max", grp, it, n) for it in items for n in range(NCH)]

    HEAD_ORDER = [1, 2, 3, 0]
    SPREAD = {1: (4, 4, 4, 5, 4, 4, 4, 4, 4, 4, 4, 5, 5, 5, 4, 0), 0: (0, 0, 4, 5, 5, 6, 5, 5, 4, 3, 4, 4, 3, 4, 3, 3)}
    QK0 = [("q0", 0), ("k0", 0), ("q0", 1), ("k0", 1)]
    PREVIOUS = {0: [("x0 reciprocal", i, 0) for i in range(2)], 1: [("x0 reciprocal", i, 0) for i in range(2, 4)],
                2: [("x0", n, 0) for n in range(NCH)], 4: [("x0 lo", 0, 0)]}
    OUT = [("out", m, n) for m in range(CT) for n in range(NCH)]
    NEXT_NORM = {10: [("lo", 0, 0)], 14: [("lo", 0, 1)]}
    QUOTIENTS = {11: [("quotient", 0, 0, 0)], 12: [("quotient", 0, 0, 1)],
                 13: [("quotient", 0, 0, 2)], 15: [("heads", 0, 0)],
                 18: [("quotient", 0, 1, 0), ("quotient", 0, 1, 1)],
                 19: [("quotient", 0, 1, 2)], 20: [("heads", 0, 1)],
                 25: [("quotient", 1, 0, i) for i in range(3)], 26: [("heads", 1, 0)],
                 31: [("scale", 1, 0, i) for i in range(3)]}

    def loop_segments(more, previous):
        maxima1 = maxima(1, [j * KT + t for j in HEAD_ORDER for t in range(KT)])
        maxima0 = maxima(0, range(ITEMS))
        segments = {}
        for s in range(STEPS):
            segments[s] = [maxima1.pop(0) for _ in range(SPREAD[1][s])]
            if s == STEPS - 1:
                segments[s].append(("turn", 1))
            if previous:
                segments[s] += {5: OUT[:CT], 6: OUT[CT:]}.get(s, [])
            if more:
                segments[s] += {3: [("mean", 0, 0)], 5: [("var", 0, 0)], 7: [("mean", 0, 1)], 10: [("var", 0, 1)],
                                11: [QK0[0]], 13: [QK0[1]], 14: [QK0[2]], 15: [QK0[3]]}.get(s, [])
        for s in range(STEPS):
            segments[STEPS + s] = [maxima0.pop(0) for _ in range(SPREAD[0][s])] if more else []
            segments[STEPS + s] += {11: [("proj", 0, m) for m in range(CT)], 12: [("mean", 1, 0)]}.get(s, [])
            if s == 14:
                segments[STEPS + s].insert(2, ("var", 1, 0))
        segments["turn"] = maxima0 + [("turn", 0)] if more else []
        segments["proj"] = [("proj", 1, m) for m in range(CT)]
        segments["mean2"] = [("mean", 1, 1)]
        segments["var2"] = [("var", 1, 1)]
        segments["layer1"] = maxima(2, range(KT))
        segments["turn1"] = [("turn", 2)]
        return segments

    FIRST = Plan(list(NEXT),
                 {"mean": [("mean", 0, 0)], "mean, var": [("var", 0, 0), ("mean", 0, 1)], "var": [("var", 0, 1)],
                  "qk": QK0, "maxima": maxima(0, range(ITEMS)) + [("turn", 0)]}, [0], previous=False)
    before = dict(jobs_before=len(FIRST.jobs), places_before=len(FIRST.places))
    START = Plan(LOOP_JOBS, loop_segments(True, False), [1, 0, 2], previous=False, uses_before=len(FIRST.uses), **before)
    before.update(uses_before=len(FIRST.uses) - len(OUT))
    LOOP = Plan(LOOP_JOBS, loop_segments(True, True), [1, 0, 2], **before)
    LAST = Plan([j for j in LOOP_JOBS if j not in NEXT], loop_segments(False, True), [1, 2], more=False, **before)
    FINISH = Plan([], {"out": OUT}, [], uses_before=LAST.uses_before + len(LAST.uses) - len(LOOP.uses))

    def job_done(pl, it, name):
        return pl.jobs_before + it * NJ + pl.jobs.index(name) + 1

    def uses_up_to(pl, it, use):
        return pl.uses_before + it * len(LOOP.uses) + pl.uses.index(use) + 1

    def place_no(pl, it, grp):
        return pl.places_before + it * len(LOOP.places) + pl.places.index(grp) + 1

    def image_next(pl, it):
        return 0 if pl is FIRST else it + 1

    with ExitStack() as ctx:
        def sb(name, shape, dt=F32):
            return ctx.enter_context(nc.sbuf_tensor(name, shape, dt))

        def sem(name):
            return ctx.enter_context(nc.semaphore(name))

        wqkv_s = sb("wqkv_s", [P, 2, CT, 3 * C], F32R)
        wproj_s = sb("wproj_s", [P, 2, CT, C], F32R)
        w1_s = sb("w1_s", [P, 2, CT, HID], F32R)
        w2_s = sb("w2_s", [P, 2, HT, C], F32R)
        wfhg_s = sb("wfhg_s", [P, 2, CT, 7 * DH], F32R)
        wv_s = sb("wv_s", [3 * DH, C], F32R)
        vec = sb("vec", [P, V_COLS])
        bias = sb("bias", [P, B_COLS])
        avg = sb("avg", [P, P])
        ones = sb("ones", [P, DH])
        ident = sb("ident", [P, P])
        three_halves = sb("three_halves", [P, 1])
        xin = sb("xin", [P, CT, N])
        y = sb("y", [P, CT, N])
        xc = sb("xc", [P, CT, N])
        sq = sb("sq", [P, CT, N])
        nrm = sb("nrm", [P, 2, CT, N], F32R)
        act = sb("act", [P, 2, CT, N], F32R)
        qs = sb("qs", [P, HEADS, N], F32R)
        ks = sb("ks", [P, HEADS, N], F32R)
        vals = sb("vals", [P, KT, C])
        vals1 = sb("vals1", [P, KT, DH])
        pr = sb("pr", [P, 4, 2, CH])
        mx = sb("mx", [P, NCH, ITEMS])
        mxc = sb("mxc", [P, ITEMS])
        negm = sb("negm", [ITEMS, P], F32R)
        hid_hi = ks[:, G:2 * G, :].rearrange("p a (b c) -> p (a b) c", c=CH)
        hid_lo = qs[:, G:2 * G, :].rearrange("p a (b c) -> p (a b) c", c=CH)
        q0_stage, k0_stage = xc[:, :, :].bitcast(F32R), y[:, :, :].bitcast(F32R)
        stage1 = act[:, :, :, :].rearrange("p a t n -> p (a t) n")
        f_stack, g_stack = qs[:, G, :], ks[:, G, :]
        x0s = qs[0:3 * DH, G, :]
        quot = sq[:, 0, 0:CH]
        den = sq[:, 1, 0:CH]

        def guess(g, n):
            return y[:, 0, 0:CH] if g + n == 0 else sq[:, 0, CH:2 * CH]

        att_copy, x0_recips = den, quot
        x0 = sq[0:DH, :, CH:2 * CH]
        h_rows = sq[NEG:P, 0, :]

        maxp = ctx.enter_context(nc.psum_tensor("maxp", [P, 2, CH], F32))
        lin = ctx.enter_context(nc.psum_tensor("lin", [P, 3, 2, CH], F32))
        att_o, att_d = lin[:, 2, 0, :], lin[:, 2, 1, :]

        vec_loaded = sem("vec_loaded")
        weights_loaded = sem("weights_loaded")
        consts_zeroed = sem("consts_zeroed")
        consts_ready = sem("consts_ready")
        bias_sums = sem("bias_sums")
        bias_ready = sem("bias_ready")
        split_step = sem("split_step")
        weights_ready = sem("weights_ready")
        x_next_loaded = sem("x_next_loaded")
        x_loaded = sem("x_loaded")
        squared = [sem(f"squared{k}") for k in range(2)]
        log_ready = [sem(f"log_ready{k}") for k in range(2)]
        inputs_added = [sem(f"inputs_added{k}") for k in range(2)]
        squares_added = [sem(f"squares_added{k}") for k in range(2)]
        guess_ready = [sem(f"guess_ready{k}") for k in range(2)]
        newton = [sem(f"newton{k}") for k in range(2)]
        normed = [sem(f"normed{k}") for k in range(2)]
        normed_hi = [sem(f"normed_hi{k}") for k in range(2)]
        norm_split = [sem(f"norm_split{k}") for k in range(2)]
        job_ready = sem("job_ready")
        ring_ready = sem("ring_ready")
        ring_read = sem("ring_read")
        qk0_hi = sem("qk0_hi")
        qk1_hi = sem("qk1_hi")
        qk1_staged = sem("qk1_staged")
        head_stacked = [[sem(f"head_stacked{grp}_{j}") for j in range(G)] for grp in range(GROUPS)]
        max_ready = sem("max_ready")
        negm_placed = sem("negm_placed")
        ones_ready = sem("ones_ready")
        scores_ready = sem("scores_ready")
        exp_done = sem("exp_done")
        pv_done = sem("pv_done")
        vals_ready = sem("vals_ready")
        h_copied = sem("h_copied")
        vals1_ready = sem("vals1_ready")
        sums_copied = sem("sums_copied")
        den_log = sem("den_log")
        den_guess = sem("den_guess")
        recip_step = sem("recip_step")
        quot_ready = sem("quot_ready")
        quot_hi = sem("quot_hi")
        heads_ready = sem("heads_ready")
        y_free = sem("y_free")
        hid_ready = sem("hid_ready")
        hid_hi_ready = sem("hid_hi_ready")
        hid_split = sem("hid_split")
        y2_ready = sem("y2_ready")
        y2_hi = sem("y2_hi")
        y2_split = sem("y2_split")
        fg_hi = sem("fg_hi")
        fg_stacked = sem("fg_stacked")
        x0_recip = sem("x0_recip")
        x0_ready = sem("x0_ready")
        x0_hi = sem("x0_hi")
        x0_split = sem("x0_split")
        att_copied = sem("att_copied")

        READ = {}
        for w in range(2):
            READ[f"vals{w}"] = (vals_ready, w + 1, 2)
            READ[f"down{w}"] = (y2_ready, CT * (w + 1), NCH * CT)
        for i in range(8):
            READ[f"up{i // 4}_{i % 4}"] = (hid_ready, 2 * i + 2, 16)
        READ["q1"], READ["k1"] = (qk1_staged, 1, 2), (qk1_staged, 2, 2)
        READ["f"], READ["g"], READ["h"] = (fg_stacked, 1, 2), (fg_stacked, 2, 2), (vals1_ready, 1, 1)

        def wait_read(eng, pl, it, name):
            signal, value, per_image = READ[name]
            eng.wait_ge(signal, (image_next(pl, it) if name in NEXT else it) * per_image + value)

        def wait_pair(eng, pl, it, name):
            before = [j for j in pl.jobs[:pl.jobs.index(name)] if PAIR[j] == PAIR[name]]
            if before:
                wait_read(eng, pl, it, before[-1])

        def wait_stacked(eng, image, grp, head):
            eng.wait_ge(head_stacked[grp][head], (image + 1) * STACK)

        def pair(name):
            return lin[:, PAIR[name], :, :]

        def columns(n):
            return slice(n * CH, n * CH + CH)

        def mean_temp(k, n):
            return sq[:, 0, 0:CH] if k == 0 else sq[:, 0, temps(k, n)]

        def norm_source(k):
            return xc if k == 0 else y

        def temps(k, n):
            return columns(1 if k == 0 else 1 - n)

        raw_qkv = y[:, :, 0:3 * C]
        raw_w1 = xc[:, :, :]
        prf = pr[:, :, :, :].rearrange("p a b c -> p (a b c)")
        raw_w2 = prf[:, 0:HT * C].rearrange("p (t c) -> p t c", c=C)
        raw_proj = prf[:, 2048:2048 + CT * C].rearrange("p (t c) -> p t c", c=C)
        raw_fgh = prf[:, 2560:2560 + CT * 3 * DH].rearrange("p (t c) -> p t c", c=3 * DH)
        raw_wv = prf[0:3 * DH, 2816:2816 + C]
        scaled_wv = prf[0:3 * DH, 3072:3072 + C]

        block = ctx.enter_context(nc.Block())

        @block.sync
        def _(sp):
            sp.dma_start(vec[:, :], vecs).then_inc(vec_loaded, DMA)
            for t in range(CT):
                rows = slice(t * P, t * P + P)
                sp.dma_start(raw_qkv[:, t, :], wqkv[rows, :]).then_inc(weights_loaded, DMA)
                sp.dma_start(raw_w1[:, t, :], w1[rows, :]).then_inc(weights_loaded, DMA)
                sp.dma_start(raw_proj[:, t, :], wproj[rows, :]).then_inc(weights_loaded, DMA)
                sp.dma_start(raw_fgh[:, t, :], wfgh[rows, :]).then_inc(weights_loaded, DMA)
            sp.dma_start(raw_w2, w2.rearrange("(t p) c -> p t c", p=P)).then_inc(weights_loaded, DMA)
            for r in range(3):
                sp.dma_start(raw_wv[r * DH:r * DH + DH, :], wv).then_inc(weights_loaded, DMA)
            sp.sem_inc(y_free, 1)

            def stack(grp, parts, heads):
                for j in heads:
                    for dst, order in ((qs, (0, 1, 0)), (ks, (2, 2, 3))):
                        for r, part in enumerate(order):
                            sp.dma_start(dst[r * DH:r * DH + DH, G * grp + j, :].bitcast(F32),
                                         parts[part][j * DH:j * DH + DH, :]).then_inc(head_stacked[grp][j], DMA)

            stage1_parts = [stage1[:, i, :].bitcast(F32) for i in range(4)]

            def stack0():
                stack(0, (xc[:, 0, :], xc[:, 1, :], y[:, 0, :], y[:, 1, :]), range(G))

            def stack1(pl, it, heads):
                sp.wait_ge(qk1_staged, image_next(pl, it) * 2 + 2)
                stack(1, stage1_parts, heads)

            def place_negm(pl, it, grp):
                n = ITEMS if grp < 2 else KT
                sp.wait_ge(ring_read, uses_up_to(pl, it, ("turn", grp)))
                row = qs[NEG:NEG + 1, G * grp:G * grp + G, :] if grp < 2 else qs[NEG:NEG + 1, G:G + 1, :]
                sp.dma_start(row.bitcast(F32).rearrange("p a (b c) -> p (a b) c", c=P),
                             negm[0:n, :].bitcast(F32)).then_inc(negm_placed, DMA)

            def load_next(image):
                sp.dma_start(xc[:, :, :], x[bass.ds(image, 1), :, :].rearrange("a (t p) n -> p (a t) n", p=P)
                             ).then_inc(x_next_loaded, DMA)

            def image(pl, it, ahead=True):
                if pl.previous:
                    store(pl, it)
                    stack(1, stage1_parts, [0])
                place_negm(pl, it, 1)
                if pl.more:
                    sp.wait_ge(ring_read, uses_up_to(pl, it, QK0[-1]))
                    stack0()
                    place_negm(pl, it, 0)
                    sp.wait_ge(norm_split[1], it * NCH + NCH)
                    if ahead:
                        load_next(it + 2)
                    following = x[bass.ds(it + 1, 1), :, :].rearrange("a (t p) n -> p (a t) n", p=P)
                    sp.dma_start(xin[:, :, :], following).then_inc(x_loaded, DMA)
                sp.wait_ge(job_ready, job_done(pl, it, "down1"))
                sp.dma_start(ks[NEG:NEG + 1, G:2 * G, :].bitcast(F32), ks[NEG:NEG + 1, 0:G, :].bitcast(F32)
                             ).then_inc(ones_ready, DMA)
                place_negm(pl, it, 2)
                if pl.more:
                    stack1(pl, it, range(1, G))

            def store(pl, it):
                for m in range(CT):
                    sp.wait_ge(ring_read, uses_up_to(pl, it, ("out", m, NCH - 1)))
                    sp.dma_start(out[bass.ds(it - 1, 1), m * P:m * P + P, :].rearrange("a p n -> p (a n)"),
                                 y[:, m, :]).then_inc(y_free, DMA)

            sp.wait_ge(weights_ready, 1)
            for dst, signal in ((xc, x_next_loaded), (xin, x_loaded)):
                sp.dma_start(dst[:, :, :], x[0, :, :].rearrange("(t p) n -> p t n", p=P)).then_inc(signal, DMA)
            sp.wait_ge(ring_read, uses_up_to(FIRST, 0, ("k0", NCH - 1)))
            stack0()
            stack1(FIRST, 0, HEAD_ORDER)
            place_negm(FIRST, 0, 0)
            for j in range(G):
                wait_stacked(sp, 0, 0, j)
            load_next(1)
            image(START, 0)
            with sp.Fori(1, IMGS - 2) as it:
                image(LOOP, it)
            image(LOOP, IMGS - 2, ahead=False)
            image(LAST, IMGS - 1)
            store(FINISH, IMGS)
            sp.wait_ge(y_free, 1 + IMGS * CT * DMA)

        @block.gpsimd
        def _(pool):
            nc.gpsimd.memset(avg[:, :], 1.0 / C).then_inc(consts_ready, 1)
            nc.gpsimd.memset(ones[:, :], 1.0).then_inc(consts_ready, 1)
            nc.gpsimd.memset(three_halves[:, :], 1.5).then_inc(consts_ready, 1)
            pool.wait_ge(consts_ready, 3)
            nc.gpsimd.memset(ks[NEG:NEG + 1, :, :].bitcast(F32), 1.0).then_inc(ones_ready, 1)
            pool.wait_ge(ones_ready, 1)
            nc.gpsimd.memset(ident[:, :], 0.0).then_inc(consts_zeroed, 1)
            pool.wait_ge(consts_zeroed, 1)
            nc.gpsimd.affine_select(out=ident[:, :], in_=ident[:, :], compare_op=ALU.not_equal, fill=1.0, base=0,
                                    pattern=[[-1, P]], channel_multiplier=1).then_inc(consts_ready, 1)

            def add_inputs(k, image, n):
                src = norm_source(k)
                nc.gpsimd.tensor_tensor(mean_temp(k, n), src[:, 0, columns(n)], src[:, 1, columns(n)],
                                        ALU.add).then_inc(inputs_added[k], 1)

            def add_squares(k, image, n):
                a, b = sq[:, 0, temps(k, n)], sq[:, 1, temps(k, n)]
                pool.wait_ge(squared[k], image * NCH + n + 1)
                nc.gpsimd.tensor_tensor(a, a, b, ALU.add).then_inc(squares_added[k], 1)

            def scale(image, n):
                a, r = sq[:, 0, temps(0, n)], sq[:, 1, temps(0, n)]
                turn = image * NCH + n
                pool.wait_ge(guess_ready[0], turn + 1)
                nc.gpsimd.tensor_tensor(a, a, r, ALU.mult).then_inc(newton[0], 1)
                pool.wait_ge(newton[0], turn * 4 + 1)
                nc.gpsimd.tensor_tensor(a, a, r, ALU.mult).then_inc(newton[0], 1)
                pool.wait_ge(newton[0], turn * 4 + 2)
                nc.gpsimd.tensor_tensor(a, a, three_halves[:, 0:1].to_broadcast([P, CH]), ALU.add).then_inc(newton[0], 1)
                pool.wait_ge(newton[0], turn * 4 + 3)
                nc.gpsimd.tensor_tensor(a, a, r, ALU.mult).then_inc(newton[0], 1)
                pool.wait_ge(newton[0], turn * 4 + 4)
                for t in range(CT):
                    last = nc.gpsimd.tensor_tensor(xc[:, t, columns(n)], xc[:, t, columns(n)], a, ALU.mult)
                last.then_inc(normed[0], 1)

            def first_norm(pl, it):
                image = image_next(pl, it)
                if pl.previous:
                    pool.wait_ge(x0_ready, it * NCH)
                pool.wait_ge(x_next_loaded, (image + 1) * DMA)
                add_inputs(0, image, 0)
                add_squares(0, image, 0)
                pool.wait_ge(ring_read, uses_up_to(pl, it, ("mean", 0, 0)))
                add_inputs(0, image, 1)
                scale(image, 0)
                add_squares(0, image, 1)
                scale(image, 1)

            def image(pl, it):
                if pl.more:
                    first_norm(pl, it)
                for n in range(NCH):
                    pool.wait_ge(ring_read, uses_up_to(pl, it, ("proj", n, CT - 1)))
                    add_inputs(1, it, n)
                    add_squares(1, it, n)

            first_norm(FIRST, 0)
            image(START, 0)
            with pool.Fori(1, IMGS - 1) as it:
                image(LOOP, it)
            image(LAST, IMGS - 1)

        @block.tensor
        def _(pe):
            pe.wait_ge(vec_loaded, DMA)
            pe.wait_ge(weights_loaded, 12 * DMA)
            pe.wait_ge(consts_ready, 4)
            for o in range(3 * CT):
                for t in range(CT):
                    pe.matmul(maxp[:, 0, o:o + 1], raw_qkv[:, t, o * P:o * P + P],
                              vec[:, V_BETA1 + t:V_BETA1 + t + 1], start=t == 0, stop=t == CT - 1)
            for o in range(HT):
                for t in range(CT):
                    pe.matmul(maxp[:, 0, B_FFN + o:B_FFN + o + 1], raw_w1[:, t, o * P:o * P + P],
                              vec[:, V_BETA2 + t:V_BETA2 + t + 1], start=t == 0, stop=t == CT - 1)
            for o in range(CT):
                last = pe.matmul(maxp[:, 0, B_OUT + o:B_OUT + o + 1], raw_wv[0:DH, o * P:o * P + P],
                                 vec[0:DH, V_BH:V_BH + 1], start=True, stop=True)
            last.then_inc(bias_sums, 1)
            pe.wait_ge(bias_ready, 1)
            for o in range(CT):
                for t in range(CT):
                    last = pe.matmul(maxp[:, 1, o:o + 1], raw_proj[:, t, o * P:o * P + P],
                                     bias[:, B_V + t:B_V + t + 1], start=t == 0, stop=t == CT - 1)
            last.then_inc(bias_sums, 1)
            pe.wait_ge(weights_ready, 1)

            def triple(dst, w, cols, src, tok, tiles, parts=range(3 * CT)):
                products = [(t, a, b) for t in tiles for a, b in ((HI, HI), (LO, HI), (HI, LO))]
                for i in parts:
                    t, a, b = products[i]
                    last = pe.matmul(dst, w[:, a, t, cols], src[:, b, t, tok], start=i == 0, stop=i == len(products) - 1)
                return last


            def projection(name, w, cols, src, chunks=range(NCH)):
                m = cols.stop - cols.start
                for n in chunks:
                    last = triple(pair(name)[0:m, n, :], w, cols, src, columns(n), range(CT))
                if n == NCH - 1:
                    last.then_inc(job_ready, 1)

            def keys_first(dst, src, k, w):
                n_mm = 0
                for t in range(CT):
                    for a, b in ((HI, HI), (LO, HI), (HI, LO)):
                        last = pe.matmul(dst, src[:, a, t, k * P:k * P + P], w[:, b, t, :],
                                         start=n_mm == 0, stop=n_mm == 3 * CT - 1)
                        n_mm += 1
                return last

            def values(half):
                for i in range(4):
                    last = keys_first(pair(f"vals{half}")[:, i // 2, (i % 2) * C:(i % 2) * C + C], nrm, 4 * half + i,
                                      wqkv_s[:, :, :, 2 * C:3 * C])
                last.then_inc(job_ready, 1)

            def ring(pl, it, segment, part=0, parts=1):
                uses = pl.segments[segment]
                for use in [uses[i] for i in split_evenly(len(uses), parts, part)]:
                    kind, idx = use[0], pl.uses.index(use)
                    bank = maxp[:, idx % 2, :]
                    before = uses_up_to(pl, it, use) - 1
                    if idx == 0 and pl is not FIRST:
                        pe.wait_ge(ring_read, before)
                    elif idx > 0 and (pl is not FIRST or idx > 1):
                        pe.wait_ge(ring_read, before - 1)
                    image = image_next(pl, it)
                    if kind == "max":
                        _, grp, item, n = use
                        j, t = item // KT, item % KT
                        if grp < 2:
                            if item % KT == 0 and n == 0:
                                wait_stacked(pe, image if grp == 0 else it, grp, j)
                            q, k = qs[0:NEG, G * grp + j, :], ks[0:NEG, G * grp + j, :]
                        else:
                            q, k = f_stack[0:NEG], g_stack[0:NEG]
                        last = pe.matmul(bank, q[:, t * P:t * P + P], k[:, columns(n)], start=True, stop=True)
                    elif kind == "turn":
                        n = ITEMS if use[1] < 2 else KT
                        pe.wait_ge(max_ready, place_no(pl, it, use[1]))
                        last = pe.transpose(bank[0:n, 0:P], mxc[:, 0:n], ident[:, :])
                    elif kind == "mean":
                        _, k, n = use
                        pe.wait_ge(inputs_added[k], (image if k == 0 else it) * NCH + n + 1)
                        last = pe.matmul(bank, avg[:, :], mean_temp(k, n), start=True, stop=True)
                    elif kind == "var":
                        _, k, n = use
                        pe.wait_ge(squares_added[k], (image if k == 0 else it) * NCH + n + 1)
                        last = pe.matmul(bank, avg[:, :], sq[:, 0, temps(k, n)], start=True, stop=True)
                    elif kind == "out":
                        _, m, n = use
                        pe.wait_ge(x0_split, it)
                        last = pe.matmul(bank, wv_s[:, m * P:m * P + P], x0s[:, columns(n)], start=True, stop=True)
                    elif kind == "proj":
                        _, n, m = use
                        if m == 0:
                            pe.wait_ge(heads_ready, it * 4 + 3 + n)
                        last = triple(bank, wproj_s, slice(m * P, m * P + P), act, columns(n), range(CT))
                    else:
                        first = 0 if kind == "q0" else C
                        pe.wait_ge(norm_split[0], image * NCH + use[1] + 1)
                        last = triple(bank, wqkv_s, slice(first, first + P), nrm, columns(use[1]), range(CT))
                    last.then_inc(ring_ready, 1)

            def half_scores(pl, it, idx, cols):
                if idx >= 2 or pl.previous:
                    pe.wait_ge(exp_done, it * HALVES + idx - 1)
                for i, (k, kt, q, n) in enumerate(cols):
                    last = pe.matmul(lin[:, idx % 2, i, :], k[0:NEG + 1, kt * P:kt * P + P],
                                     q[0:NEG + 1, columns(n)], start=True, stop=True)
                last.then_inc(scores_ready, 1)

            def step_scores(pl, it, g, s, p):
                n, kt = s // KT, s % KT
                heads = [G * g + 2 * p + i for i in range(2)]
                half_scores(pl, it, (g * STEPS + s) * 2 + p, [(ks[:, h, :], kt, qs[:, h, :], n) for h in heads])

            def step_pv(pl, it, g, s, between=lambda i: None):
                n, kt = s // KT, s % KT
                idx = (g * STEPS + s) * 2
                pe.wait_ge(exp_done, it * HALVES + idx + 2)
                if g + s == 0 and pl.previous:
                    pe.wait_ge(att_copied, it)
                elif kt == 0 and g + n > 0:
                    pe.wait_ge(sums_copied, it * 4 + 2 * g + n)
                for j in range(G):
                    if j == G // 2:
                        between(0)
                    pe.matmul(att_o[j * DH:j * DH + DH, :], vals[:, kt, (G * g + j) * DH:(G * g + j + 1) * DH],
                              pr[:, (idx + j // 2) % 4, j % 2, :], start=kt == 0, stop=kt == KT - 1)
                between(1)
                for j in range(G):
                    if j == G // 2:
                        between(2)
                    last = pe.matmul(att_d[j * DH:j * DH + DH, :], ones[:, :],
                                     pr[:, (idx + j // 2) % 4, j % 2, :], start=kt == 0, stop=kt == KT - 1)
                last.then_inc(pv_done, 1)

            def hidden_up(name, n, j):
                for i in range(2):
                    m = 2 * j + i
                    last = triple(pair(name)[:, i, :], w1_s, slice(m * P, m * P + P), act, columns(n), range(CT))
                last.then_inc(job_ready, 1)

            def hidden_down(it, n, beside=lambda: None):
                name = f"down{n}"
                for k in range(HT):
                    if k == 3:
                        beside()
                    if k % 2 == 0:
                        pe.wait_ge(hid_split, it * 2 * 4 + n * 4 + k // 2 + 1)
                    for m in range(CT):
                        for i, (a, b) in enumerate(((HI, hid_hi), (LO, hid_hi), (HI, hid_lo))):
                            last = pe.matmul(pair(name)[:, m, :], w2_s[:, a, k, m * P:m * P + P], b[:, k, :],
                                             start=k == 0 and i == 0, stop=k == HT - 1 and i == 2)
                last.then_inc(job_ready, 1)

            def image(pl, it):
                pe.wait_ge(negm_placed, (pl.places_before + it * len(LOOP.places)) * DMA)
                pe.wait_ge(vals_ready, it * 2 + 2)
                for s in range(GROUPS * STEPS):
                    def beside(part):
                        if s != STEPS - 1:
                            ring(pl, it, s, part, 6)
                        elif part == 1:
                            ring(pl, it, s)

                    if s == STEPS:
                        pe.wait_ge(negm_placed, place_no(pl, it, 1) * DMA)
                    for p in range(2):
                        step_scores(pl, it, s // STEPS, s % STEPS, p)
                        beside(p)
                    if s > 0:
                        step_pv(pl, it, (s - 1) // STEPS, (s - 1) % STEPS, lambda i: beside(2 + i))
                    else:
                        for i in range(3):
                            beside(2 + i)
                    beside(5)
                step_pv(pl, it, GROUPS - 1, STEPS - 1)

                def up(n, j):
                    wait_pair(pe, pl, it, f"up{n}_{j}")
                    hidden_up(f"up{n}_{j}", n, j)

                pe.wait_ge(exp_done, it * HALVES + L0_HALVES)
                if pl.more:
                    values(0)
                    ring(pl, it, "turn", 0, 4)
                    values(1)
                    ring(pl, it, "turn", 1, 4)
                pe.wait_ge(sums_copied, it * 4 + 4)
                pe.wait_ge(norm_split[1], it * NCH + 1)
                up(0, 0)
                ring(pl, it, "turn", 2, 4)
                up(0, 1)
                ring(pl, it, "turn", 3, 4)
                up(0, 2)
                ring(pl, it, "proj")
                up(0, 3)
                ring(pl, it, "mean2")
                wait_pair(pe, pl, it, "down0")
                hidden_down(it, 0, lambda: ring(pl, it, "var2"))
                pe.wait_ge(norm_split[1], it * NCH + NCH)
                for j in range(4):
                    up(1, j)
                wait_pair(pe, pl, it, "down1")
                hidden_down(it, 1)

                wait_pair(pe, pl, it, "f")
                wait_pair(pe, pl, it, "g")
                for n in range(NCH):
                    pe.wait_ge(y2_split, it * NCH + n + 1)
                    projection("f", wfhg_s, slice(0, 4 * DH), act, [n])
                    projection("g", wfhg_s, slice(4 * DH, 7 * DH), act, [n])
                    if pl.more:
                        if n == 0:
                            wait_pair(pe, pl, it, "q1")
                        projection("q1", wqkv_s, slice(P, C), nrm, [n])
                pe.wait_ge(fg_stacked, it * 2 + 2)
                for i in range(8):
                    ring(pl, it, "layer1", i, 8)
                    if i == 3:
                        pe.wait_ge(h_copied, it + 1)
                        wait_pair(pe, pl, it, "h")
                        for k in range(KT):
                            last = pe.matmul(pair("h")[:, 0, k * DH:k * DH + DH], h_rows[:, k * P:k * P + P],
                                             ident[NEG:P, NEG:P], start=True, stop=True)
                        last.then_inc(job_ready, 1)
                    if pl.more and i < 7 and i != 3:
                        if i == 0:
                            wait_pair(pe, pl, it, "k1")
                        part = i if i < 3 else i - 1
                        n = part // 3
                        last = triple(pair("k1")[:, n, :], wqkv_s, slice(C + P, 2 * C), nrm, columns(n), range(CT),
                                      range(part % 3 * 2, part % 3 * 2 + 2))
                        if part == 5:
                            last.then_inc(job_ready, 1)
                ring(pl, it, "turn1")
                wait_read(pe, pl, it, "h")
                pe.wait_ge(ones_ready, 1 + (it + 1) * DMA)
                pe.wait_ge(negm_placed, place_no(pl, it, 2) * DMA)
                for kt in range(KT + 1):
                    if kt == 1 and pl.more:
                        wait_read(pe, pl, it, "k1")
                    if kt < KT:
                        half_scores(pl, it, L0_HALVES + kt, [(g_stack, kt, f_stack, n) for n in range(NCH)])
                    if kt > 0:
                        k = kt - 1
                        idx = L0_HALVES + k
                        pe.wait_ge(exp_done, it * HALVES + idx + 1)
                        for n in range(NCH):
                            pe.matmul(att_o[n * DH:n * DH + DH, :], vals1[:, k, :], pr[:, idx % 4, n, :],
                                      start=k == 0, stop=k == KT - 1)
                        for n in range(NCH):
                            last = pe.matmul(att_o[2 * DH + n * DH:3 * DH + n * DH, :], ones[:, :], pr[:, idx % 4, n, :],
                                             start=k == 0, stop=k == KT - 1)
                        last.then_inc(pv_done, 1)

            pe.wait_ge(ones_ready, 1)
            for segment in ("mean", "mean, var", "var", "qk"):
                ring(FIRST, 0, segment)
            values(0)
            values(1)
            wait_pair(pe, FIRST, 0, "q1")
            projection("q1", wqkv_s, slice(P, C), nrm)
            wait_pair(pe, FIRST, 0, "k1")
            projection("k1", wqkv_s, slice(C + P, 2 * C), nrm)
            ring(FIRST, 0, "maxima")
            wait_read(pe, FIRST, 0, "k1")
            image(START, 0)
            with pe.Fori(1, IMGS - 1) as it:
                image(LOOP, it)
            image(LAST, IMGS - 1)
            ring(FINISH, IMGS, "out")

        @block.scalar
        def _(sc):
            sc.preload_act_table_set("natural_log_exp_and_others")
            sc.wait_ge(weights_ready, 1)
            sc.wait_ge(consts_ready, 4)

            def norm_square(pl, it, k, n):
                image = image_next(pl, it) if k == 0 else it
                sc.wait_ge(ring_read, uses_up_to(pl, it, ("mean", k, n)))
                nc.scalar.activation(sq[:, :, temps(k, n)], xc[:, :, columns(n)], ACT.Square).then_inc(squared[k], 1)

            def norm_guess(pl, it, k, n):
                image = image_next(pl, it) if k == 0 else it
                var, guess = sq[:, 0, temps(k, n)], sq[:, 1, temps(k, n)]
                sc.wait_ge(ring_read, uses_up_to(pl, it, ("var", k, n)))
                nc.scalar.activation(guess, var, ACT.Ln, scale=-2.0).then_inc(log_ready[k], 1)
                sc.wait_ge(log_ready[k], image * NCH + n + 1)
                nc.scalar.activation(guess, guess, ACT.Exp, scale=-0.5).then_inc(guess_ready[k], 1)

            def norm_hi(pl, it, k, n):
                image = image_next(pl, it) if k == 0 else it
                dst = nrm if k == 0 else act
                sc.wait_ge(normed[k], image * NCH + n + 1)
                nc.scalar.copy(dst[:, HI, :, columns(n)], xc[:, :, columns(n)]).then_inc(normed_hi[k], 1)

            def qk0_evac(pl, it, name, n):
                dst, col = (q0_stage, B_QK) if name == "q0" else (k0_stage, B_QK + 2)
                use = (name, n)
                if use == QK0[1] and pl is not FIRST:
                    sc.wait_ge(recip_step, it * 8 + 2)
                sc.wait_ge(ring_ready, uses_up_to(pl, it, use))
                nc.scalar.activation(dst[:, 0, columns(n)], maxp[:, pl.uses.index(use) % 2, :], ACT.Identity,
                                     bias=bias[:, col:col + 1]).then_inc(qk0_hi, 1)

            def qk1_evac(pl, it, name):
                slot, col = (0, B_QK + 1) if name == "q1" else (2, B_QK + 3)
                sc.wait_ge(job_ready, job_done(pl, it, name))
                nc.scalar.activation(stage1[:, slot, :], pair(name), ACT.Identity,
                                     bias=bias[:, col:col + 1]).then_inc(qk1_hi, 1)

            def vals_evac(pl, it, half):
                sc.wait_ge(job_ready, job_done(pl, it, f"vals{half}"))
                nc.scalar.copy(vals[:, 4 * half:4 * half + 4, :], pair(f"vals{half}")).then_inc(vals_ready, 1)

            def copy_att(it):
                sc.wait_ge(pv_done, it * PV)
                nc.scalar.copy(att_copy, att_o).then_inc(att_copied, 1)

            def x0_split_hi(it, copy):
                sc.wait_ge(x0_ready, it * NCH)
                rows = slice(2 * copy * DH, (2 * copy + 1) * DH)
                nc.scalar.copy(x0s[rows, :].rearrange("p (a b) -> p a b", b=CH), x0).then_inc(x0_hi, 1)

            def half_exp(pl, it, idx, scale):
                sc.wait_ge(scores_ready, it * HALVES + idx + 1)
                if idx < 4:
                    if pl.previous:
                        sc.wait_ge(pv_done, it * PV - 3 + idx)
                elif idx < L0_HALVES:
                    sc.wait_ge(pv_done, it * PV + (idx - 4) // 2 + 1)
                elif idx >= L0_HALVES + 4:
                    sc.wait_ge(pv_done, it * PV + GROUPS * STEPS + idx - 4 - L0_HALVES + 1)
                nc.scalar.activation(pr[:, idx % 4, :, :], lin[:, idx % 2, :, :], ACT.Exp,
                                     scale=scale).then_inc(exp_done, 1)

            def sums_copy(it, g, n):
                sc.wait_ge(pv_done, it * PV + (g * NCH + n + 1) * KT)
                if g + n > 0:
                    sc.wait_ge(heads_ready, it * 4 + 2 * g + n)
                nc.scalar.copy(sq[:, :, 0:CH], lin[:, 2, :, :]).then_inc(sums_copied, 1)

            def den_recip(it, g, n):
                k = it * 4 + 2 * g + n
                sc.wait_ge(sums_copied, k + 1)
                if g + n == 0:
                    sc.wait_ge(y_free, it * CT * DMA + 1)
                nc.scalar.activation(guess(g, n), den, ACT.Ln).then_inc(den_log, 1)
                sc.wait_ge(den_log, k + 1)
                nc.scalar.activation(guess(g, n), guess(g, n), ACT.Exp, scale=-1.0).then_inc(den_guess, 1)

            def quot_split(it, g, n):
                if g + n == 0:
                    for j in range(G):
                        wait_stacked(sc, it, 1, j)
                sc.wait_ge(quot_ready, it * 4 + 2 * g + n + 1)
                nc.scalar.copy(act[:, HI, g, columns(n)], quot).then_inc(quot_hi, 1)

            def y2_split_hi(it, n):
                sc.wait_ge(y2_ready, it * 2 * CT + CT * (n + 1))
                nc.scalar.copy(act[:, HI, :, columns(n)], y[:, :, columns(n)]).then_inc(y2_hi, 1)

            def beside(pl, it, s, at):
                when = (s, at)
                if pl.previous:
                    if when == (0, 1):
                        copy_att(it)
                    elif when in ((3, 1), (3, 2)):
                        x0_split_hi(it, at - 1)
                if pl.more:
                    if when == (4, 2):
                        if pl.previous:
                            sc.wait_ge(x0_split, it)
                        norm_square(pl, it, 0, 0)
                    elif when == (6, 1):
                        norm_guess(pl, it, 0, 0)
                    elif when == (9, 1):
                        norm_hi(pl, it, 0, 0)
                    elif when == (9, 2):
                        norm_square(pl, it, 0, 1)
                    elif when == (11, 1):
                        norm_guess(pl, it, 0, 1)
                    elif when == (13, 2):
                        norm_hi(pl, it, 0, 1)
                    elif at == 0 and s in (12, 14, 15, 16):
                        qk0_evac(pl, it, *QK0[(12, 14, 15, 16).index(s)])
                for (g, n), copy_at, guess_at, split_at in (((0, 0), KT, (KT + 2, 1), (KT + 6, 1)),
                                                            ((0, 1), STEPS, (STEPS + 1, 1), (STEPS + 4, 1)),
                                                            ((1, 0), STEPS + KT, (STEPS + KT, 2), (STEPS + KT + 2, 1))):
                    if when == (copy_at, 2):
                        sums_copy(it, g, n)
                    if when == guess_at:
                        den_recip(it, g, n)
                    elif when == split_at:
                        quot_split(it, g, n)
                if when == (STEPS + 13, 2):
                    norm_square(pl, it, 1, 0)
                elif when == (STEPS + 14, 2):
                    norm_guess(pl, it, 1, 0)

            def hidden(pl, it, i):
                n, j = i // 4, i % 4
                hid32 = pr[:, j, :, :]
                sc.wait_ge(job_ready, job_done(pl, it, f"up{n}_{j}"))
                if i >= 4:
                    sc.wait_ge(hid_split, it * 8 + i - 3)
                for e in range(2):
                    nc.scalar.activation(hid32[:, e, :], pair(f"up{n}_{j}")[:, e, :],
                                         ACT.Relu, bias=bias[:, B_FFN + 2 * j + e:B_FFN + 2 * j + e + 1]
                                         ).then_inc(hid_ready, 1)
                sc.wait_ge(hid_ready, it * 16 + 2 * i + 2)
                if i == 4:
                    sc.wait_ge(job_ready, job_done(pl, it, "down0"))
                nc.scalar.copy(hid_hi[:, 2 * j:2 * j + 2, :], hid32).then_inc(hid_hi_ready, 1)

            def image(pl, it):
                for s in range(GROUPS * STEPS):
                    beside(pl, it, s, 0)
                    half_exp(pl, it, 2 * s, SCALE)
                    beside(pl, it, s, 1)
                    half_exp(pl, it, 2 * s + 1, SCALE)
                    beside(pl, it, s, 2)
                sums_copy(it, 1, 1)
                norm_hi(pl, it, 1, 0)
                den_recip(it, 1, 1)
                if pl.more:
                    vals_evac(pl, it, 0)
                    vals_evac(pl, it, 1)
                hidden(pl, it, 0)
                quot_split(it, 1, 1)
                hidden(pl, it, 1)
                hidden(pl, it, 2)
                hidden(pl, it, 3)
                norm_square(pl, it, 1, 1)
                norm_guess(pl, it, 1, 1)
                norm_hi(pl, it, 1, 1)
                for i in range(4, 8):
                    hidden(pl, it, i)
                y2_split_hi(it, 0)
                y2_split_hi(it, 1)
                for i, (name, dst) in enumerate((("f", f_stack), ("g", g_stack))):
                    sc.wait_ge(job_ready, job_done(pl, it, name))
                    nc.scalar.activation(dst[0:3 * DH], pair(name)[0:3 * DH], ACT.Identity,
                                         bias=vec[0:3 * DH, V_BF + i:V_BF + i + 1]).then_inc(fg_hi, 1)
                nc.scalar.copy(h_rows.rearrange("p (a b) -> p a b", b=CH), pair("f")[NEG:P]).then_inc(h_copied, 1)
                if pl.more:
                    qk1_evac(pl, it, "q1")
                sc.wait_ge(job_ready, job_done(pl, it, "h"))
                nc.scalar.copy(vals1[:, :, :], pair("h")[:, 0, 0:KT * DH].rearrange("p (a c) -> p a c", c=DH)
                               ).then_inc(vals1_ready, 1)
                if pl.more:
                    qk1_evac(pl, it, "k1")
                for kt in range(KT):
                    half_exp(pl, it, L0_HALVES + kt, 1.0)

            for n in range(NCH):
                norm_square(FIRST, 0, 0, n)
                norm_guess(FIRST, 0, 0, n)
                norm_hi(FIRST, 0, 0, n)
            for use in QK0:
                qk0_evac(FIRST, 0, *use)
            vals_evac(FIRST, 0, 0)
            vals_evac(FIRST, 0, 1)
            qk1_evac(FIRST, 0, "q1")
            qk1_evac(FIRST, 0, "k1")
            image(START, 0)
            with sc.Fori(1, IMGS - 1) as it:
                image(LOOP, it)
            image(LAST, IMGS - 1)
            copy_att(IMGS)
            for copy in range(2):
                x0_split_hi(IMGS, copy)

        @block.vector
        def _(ve):
            V = nc.vector
            ve.wait_ge(vec_loaded, DMA)
            ve.wait_ge(weights_loaded, 12 * DMA)
            ve.wait_ge(bias_sums, 1)
            V.tensor_copy(bias[:, B_QK:B_V + CT], maxp[:, 0, B_QK:B_V + CT]).then_inc(bias_ready, 1)
            V.tensor_tensor(bias[:, B_FFN:B_FFN + HT], maxp[:, 0, B_FFN:B_FFN + HT], vec[:, V_B1:V_B1 + HT], ALU.add)
            V.tensor_tensor(bias[:, B_OUT:B_OUT + CT], maxp[:, 0, B_OUT:B_OUT + CT], vec[:, V_BV:V_BV + CT],
                            ALU.add).then_inc(split_step, 1)
            ve.wait_ge(split_step, 1)
            V.tensor_scalar(bias[:, B_OUT:B_OUT + CT], bias[:, B_OUT:B_OUT + CT], vec[:, V_GAMMA:V_GAMMA + 1], None,
                            ALU.mult)
            ve.wait_ge(bias_sums, 2)
            V.tensor_tensor(bias[:, B_PROJ:B_PROJ + CT], maxp[:, 1, 0:CT], vec[:, V_BPROJ:V_BPROJ + CT], ALU.add)
            steps = 1
            for raw, dst, gain in ((raw_qkv, wqkv_s, V_G1), (raw_w1, w1_s, V_G2)):
                for t in range(CT):
                    V.tensor_scalar(raw[:, t, :], raw[:, t, :], vec[:, gain + t:gain + t + 1], None,
                                    ALU.mult).then_inc(split_step, 1)
                steps += CT
            V.tensor_scalar(scaled_wv, raw_wv, vec[0:3 * DH, V_GAMMA:V_GAMMA + 1], None, ALU.mult).then_inc(split_step, 1)
            steps += 1
            ve.wait_ge(split_step, steps)
            splits = [(raw_qkv, wqkv_s[:, :, :, :]), (raw_w1, w1_s[:, :, :, :]), (raw_w2, w2_s[:, :, :, :]),
                      (raw_proj, wproj_s[:, :, :, :])]
            splits += [(raw_fgh[:, :, i * DH:i * DH + DH], wfhg_s[:, :, :, to * DH:to * DH + DH])
                       for to, i in enumerate((0, 0, 0, 2, 1, 1, 1))]
            for raw, dst in splits:
                V.tensor_copy(dst[:, HI], raw).then_inc(split_step, 1)
            V.tensor_copy(wv_s[:, :], scaled_wv).then_inc(split_step, 1)
            steps += len(splits) + 1
            ve.wait_ge(split_step, steps)
            for raw, dst in splits:
                V.tensor_tensor(dst[:, LO], raw, dst[:, HI].bitcast(F32), ALU.subtract)
            V.tensor_tensor(wv_s[2 * DH:3 * DH, :], scaled_wv[2 * DH:3 * DH, :], wv_s[2 * DH:3 * DH, :].bitcast(F32),
                            ALU.subtract).then_inc(weights_ready, 1)

            def ring(pl, it, segment, part=0, parts=1, beside=()):
                uses = [pl.segments[segment][i] for i in split_evenly(len(pl.segments[segment]), parts, part)]
                if not uses:
                    for work in beside:
                        other(pl, it, *work)
                for place, use in enumerate(uses):
                    take(pl, it, use)
                    for i, work in enumerate(beside):
                        if i * len(uses) // len(beside) == place:
                            other(pl, it, *work)

            def other(pl, it, kind, a, b, i=0):
                if kind == "scale":
                    norm_scale(it, b, i)
                elif kind == "lo":
                    norm_lo(pl, it, a, b)
                elif kind == "quotient":
                    quotient(it, a, b, i)
                elif kind == "heads":
                    quotient_lo(it, a, b)
                elif kind == "x0 reciprocal":
                    x0_reciprocal(it, a)
                elif kind == "x0":
                    x0_quotient(it, a)
                elif kind == "x0 lo":
                    x0_lo(it)

            def x0_reciprocal(it, part):
                ve.wait_ge(att_copied, it)
                cols = slice(part * P, (part + 1) * P)
                V.reciprocal(x0_recips[0:NCH * DH, cols], att_copy[NCH * DH:2 * NCH * DH, cols]).then_inc(x0_recip, 1)

            def x0_quotient(it, n):
                ve.wait_ge(x0_recip, it * 4)
                rows = slice(n * DH, n * DH + DH)
                V.tensor_tensor(x0[:, n, :], att_copy[rows], x0_recips[rows], ALU.mult).then_inc(x0_ready, 1)

            def x0_lo(it):
                ve.wait_ge(x0_hi, it * 2)
                V.tensor_tensor(x0s[DH:2 * DH, :].rearrange("p (a b) -> p a b", b=CH), x0,
                                x0s[0:DH, :].rearrange("p (a b) -> p a b", b=CH).bitcast(F32),
                                ALU.subtract).then_inc(x0_split, 1)

            def take(pl, it, use):
                kind, idx = use[0], pl.uses.index(use)
                bank = maxp[:, idx % 2, :]
                no = uses_up_to(pl, it, use)
                if kind == "max":
                    _, grp, item, n = use
                    ve.wait_ge(ring_ready, no)
                    V.tensor_reduce(mx[:, n, item:item + 1], bank, AX.X, ALU.max).then_inc(ring_read, 1)
                    if use == [u for u in pl.uses if u[:2] == ("max", grp)][-1]:
                        m = ITEMS if grp < 2 else KT
                        ve.wait_ge(ring_read, no)
                        V.tensor_tensor(mxc[:, 0:m], mx[:, 0, 0:m], mx[:, 1, 0:m],
                                        ALU.max).then_inc(max_ready, 1)
                elif kind == "turn":
                    n = ITEMS if use[1] < 2 else KT
                    ve.wait_ge(ring_ready, no)
                    if pl is not FIRST:
                        ve.wait_ge(negm_placed, (place_no(pl, it, use[1]) - 1) * DMA)
                    V.tensor_scalar(negm[0:n, :], bank[0:n, 0:P], -1.0, None, ALU.mult).then_inc(ring_read, 1)
                elif kind == "mean":
                    n = use[2]
                    ve.wait_ge(ring_ready, no)
                    for t in range(CT):
                        last = V.tensor_tensor(xc[:, t, columns(n)], norm_source(use[1])[:, t, columns(n)], bank,
                                               ALU.subtract)
                    last.then_inc(ring_read, 1)
                elif kind == "var":
                    ve.wait_ge(ring_ready, no)
                    V.tensor_scalar(sq[:, 0, temps(*use[1:])], bank, EPS, -0.5, ALU.add, ALU.mult).then_inc(ring_read, 1)
                elif kind == "out":
                    _, m, n = use
                    ve.wait_ge(ring_ready, no)
                    V.scalar_tensor_tensor(out=y[:, m, columns(n)], in0=bank, scalar=bias[:, B_OUT + m:B_OUT + m + 1],
                                           in1=y[:, m, columns(n)], op0=ALU.add, op1=ALU.add).then_inc(ring_read, 1)
                elif kind == "proj":
                    _, n, m = use
                    if n == 0 and m == 0:
                        if pl.more:
                            for j in range(G):
                                wait_stacked(ve, it + 1, 0, j)
                        ve.wait_ge(y_free, it * CT * DMA + 1)
                        ve.wait_ge(x_loaded, it * DMA + DMA)
                    ve.wait_ge(ring_ready, no)
                    V.scalar_tensor_tensor(out=y[:, m, columns(n)], in0=bank,
                                           scalar=bias[:, B_PROJ + m:B_PROJ + m + 1], in1=xin[:, m, columns(n)],
                                           op0=ALU.add, op1=ALU.add).then_inc(ring_read, 1)
                else:
                    n = use[1]
                    dst, col = (q0_stage, B_QK) if kind == "q0" else (k0_stage, B_QK + 2)
                    ve.wait_ge(qk0_hi, image_next(pl, it) * len(QK0) + QK0.index(use) + 1)
                    V.scalar_tensor_tensor(out=dst[:, 1, columns(n)], in0=bank, scalar=bias[:, col:col + 1],
                                           in1=dst[:, 0, columns(n)].bitcast(F32),
                                           op0=ALU.add, op1=ALU.subtract).then_inc(ring_read, 1)

            def norm_scale(it, n, part):
                a, r = sq[:, 0, temps(1, n)], sq[:, 1, temps(1, n)]
                base = (it * NCH + n) * 3
                if part == 0:
                    ve.wait_ge(guess_ready[1], it * NCH + n + 1)
                    V.tensor_tensor(a, a, r, ALU.mult).then_inc(newton[1], 1)
                elif part == 1:
                    ve.wait_ge(newton[1], base + 1)
                    V.tensor_tensor(a, a, r, ALU.mult).then_inc(newton[1], 1)
                elif part == 2:
                    ve.wait_ge(newton[1], base + 2)
                    V.scalar_tensor_tensor(out=a, in0=a, scalar=1.5, in1=r, op0=ALU.add,
                                           op1=ALU.mult).then_inc(newton[1], 1)
                else:
                    t = part - 3
                    ve.wait_ge(newton[1], base + 3)
                    last = V.tensor_tensor(xc[:, t, columns(n)], xc[:, t, columns(n)], a, ALU.mult)
                    if t == CT - 1:
                        last.then_inc(normed[1], 1)

            def norm_lo(pl, it, k, n):
                image = image_next(pl, it) if k == 0 else it
                dst = nrm if k == 0 else act
                ve.wait_ge(normed_hi[k], image * NCH + n + 1)
                V.tensor_tensor(dst[:, LO, :, columns(n)], xc[:, :, columns(n)], dst[:, HI, :, columns(n)].bitcast(F32),
                                ALU.subtract).then_inc(norm_split[k], 1)

            def qk1_lo(pl, it, name):
                i, slot, col = (0, 0, B_QK + 1) if name == "q1" else (1, 2, B_QK + 3)
                ve.wait_ge(qk1_hi, image_next(pl, it) * 2 + i + 1)
                V.scalar_tensor_tensor(out=stage1[:, slot + 1, :], in0=pair(name).rearrange("p a b -> p (a b)"),
                                       scalar=bias[:, col:col + 1], in1=stage1[:, slot, :].bitcast(F32),
                                       op0=ALU.add, op1=ALU.subtract).then_inc(qk1_staged, 1)

            def quotient(it, g, n, part):
                k = it * 4 + 2 * g + n
                if part == 0:
                    ve.wait_ge(den_guess, k + 1)
                    V.tensor_tensor(den, den, guess(g, n), ALU.mult).then_inc(recip_step, 1)
                elif part == 1:
                    ve.wait_ge(recip_step, 2 * k + 1)
                    V.scalar_tensor_tensor(out=den, in0=den, scalar=-2.0, in1=guess(g, n), op0=ALU.add,
                                           op1=ALU.mult).then_inc(recip_step, 1)
                else:
                    ve.wait_ge(recip_step, 2 * k + 2)
                    V.scalar_tensor_tensor(out=quot, in0=quot, scalar=-1.0, in1=den, op0=ALU.mult,
                                           op1=ALU.mult).then_inc(quot_ready, 1)

            def quotient_lo(it, g, n):
                ve.wait_ge(quot_hi, it * 4 + 2 * g + n + 1)
                V.tensor_tensor(act[:, LO, g, columns(n)], quot, act[:, HI, g, columns(n)].bitcast(F32),
                                ALU.subtract).then_inc(heads_ready, 1)

            def hidden_lo(it, i):
                j = i % 4
                ve.wait_ge(hid_hi_ready, it * 8 + i + 1)
                V.tensor_tensor(hid_lo[:, 2 * j:2 * j + 2, :], pr[:, j, :, :],
                                hid_hi[:, 2 * j:2 * j + 2, :].bitcast(F32), ALU.subtract).then_inc(hid_split, 1)

            def feed_forward_sum(pl, it, n):
                ve.wait_ge(job_ready, job_done(pl, it, f"down{n}"))
                for m in range(CT):
                    V.scalar_tensor_tensor(out=y[:, m, columns(n)], in0=pair(f"down{n}")[:, m, :],
                                           scalar=vec[:, V_B2 + m:V_B2 + m + 1], in1=y[:, m, columns(n)],
                                           op0=ALU.add, op1=ALU.add).then_inc(y2_ready, 1)

            def image(pl, it):
                for s in range(GROUPS * STEPS):
                    ring(pl, it, s, beside=(PREVIOUS.get(s, []) if pl.previous else [])
                         + QUOTIENTS.get(s, []) + (NEXT_NORM.get(s, []) if pl.more else []))

                for part in (3, 4):
                    norm_scale(it, 0, part)
                ring(pl, it, "turn", 0, 4)
                norm_lo(pl, it, 1, 0)
                ring(pl, it, "turn", 1, 4)
                for part in range(3):
                    quotient(it, 1, 1, part)
                ring(pl, it, "turn", 2, 4)
                hidden_lo(it, 0)
                ring(pl, it, "turn", 3, 4)
                quotient_lo(it, 1, 1)
                hidden_lo(it, 1)
                hidden_lo(it, 2)
                ring(pl, it, "proj")
                hidden_lo(it, 3)
                ring(pl, it, "mean2")
                ring(pl, it, "var2")
                for part in range(5):
                    norm_scale(it, 1, part)
                norm_lo(pl, it, 1, 1)
                feed_forward_sum(pl, it, 0)
                for i in range(4, 8):
                    hidden_lo(it, i)
                y2_split_lo(it, 0)
                feed_forward_sum(pl, it, 1)
                y2_split_lo(it, 1)

                for i, (name, dst, row, col) in enumerate((("f", f_stack, 1, V_BF), ("g", g_stack, 2, V_BG))):
                    ve.wait_ge(fg_hi, it * 2 + i + 1)
                    rows = slice(row * DH, row * DH + DH)
                    V.scalar_tensor_tensor(out=dst[rows], in0=pair(name)[rows].rearrange("p a b -> p (a b)"),
                                           scalar=vec[rows, col:col + 1], in1=dst[rows].bitcast(F32),
                                           op0=ALU.add, op1=ALU.subtract).then_inc(fg_stacked, 1)
                ring(pl, it, "layer1")
                ring(pl, it, "turn1")
                if pl.more:
                    qk1_lo(pl, it, "q1")
                    qk1_lo(pl, it, "k1")

            def y2_split_lo(it, n):
                ve.wait_ge(y2_hi, it * NCH + n + 1)
                V.tensor_tensor(act[:, LO, :, columns(n)], y[:, :, columns(n)], act[:, HI, :, columns(n)].bitcast(F32),
                                ALU.subtract).then_inc(y2_split, 1)

            ve.wait_ge(weights_ready, 1)
            ring(FIRST, 0, "mean")
            ring(FIRST, 0, "mean, var")
            norm_lo(FIRST, 0, 0, 0)
            ring(FIRST, 0, "var")
            norm_lo(FIRST, 0, 0, 1)
            ring(FIRST, 0, "qk")
            qk1_lo(FIRST, 0, "q1")
            qk1_lo(FIRST, 0, "k1")
            ring(FIRST, 0, "maxima")
            image(START, 0)
            with ve.Fori(1, IMGS - 1) as it:
                image(LOOP, it)
            image(LAST, IMGS - 1)
            for works in PREVIOUS.values():
                for work in works:
                    other(FINISH, IMGS, *work)
            ring(FINISH, IMGS, "out")


def kernel(**inputs):
    import concourse.bacc as bacc
    import numpy as np
    from concourse.bass_utils import run_bass_kernel_spmd

    a = {k: np.asarray(v) for k, v in inputs.items()}
    x = np.ascontiguousarray(a["x"])
    imgs, c, hh, ww = x.shape

    def columns(v):
        v = np.tile(v, P // v.size) if v.size < P else v
        return v.reshape(-1, P).T

    vecs = np.concatenate([columns(a[n]) for n in (
        "L0_conv_g1", "L0_conv_beta1", "L0_conv_g2", "L0_conv_beta2", "L0_conv_b_proj", "L0_conv_b1", "L0_conv_b2",
        "L1_conv_bv", "L1_conv_bf", "L1_conv_bg", "L1_conv_bh", "L1_conv_gamma")], axis=1)
    arrays = {
        "x": x.reshape(imgs, c, hh * ww),
        "wqkv": a["L0_conv_w_qkv"].T,
        "wproj": a["L0_conv_w_proj"].T,
        "w1": a["L0_conv_w1"].T,
        "w2": a["L0_conv_w2"].T,
        "wfgh": np.concatenate([a["L1_conv_wf"], a["L1_conv_wg"], a["L1_conv_wh"]], axis=0).T,
        "wv": a["L1_conv_wv"].T,
        "vecs": vecs,
    }
    arrays = {f"in_{k}": np.ascontiguousarray(v) for k, v in arrays.items()}
    nc = bacc.Bacc("TRN2", target_bir_lowering=False, num_devices=1)
    args = [nc.dram_tensor(k, v.shape, F32, kind="ExternalInput").ap() for k, v in arrays.items()]
    args.append(nc.dram_tensor("out_y", (imgs, c, hh * ww), F32, kind="ExternalOutput").ap())
    attention_layers(nc, *args)
    r = run_bass_kernel_spmd(nc, [arrays], core_ids=[0])
    return r.results[0]["out_y"].reshape(x.shape)
```
